# Optimizing a Trainium2 kernel written in Bass

```python
import numpy as np
import jax
import jax.numpy as jnp

def _softmax(x, axis=-1):
    return jax.nn.softmax(x, axis=axis)

def _gelu(x):
    return jax.nn.gelu(x, approximate=True)

def _silu(x):
    return jax.nn.silu(x)

def _sigmoid(x):
    return jax.nn.sigmoid(x)

def _layernorm(x, axis=-1, eps=1e-05):
    m = jnp.mean(x, axis=axis, keepdims=True)
    v = jnp.var(x, axis=axis, keepdims=True)
    return (x - m) / jnp.sqrt(v + eps)

def _scatter_add(tgt, idx, src, axis=0):
    return tgt.at[idx].add(src)

def _segment_sum(src, seg, n):
    return jax.ops.segment_sum(src, seg, n)
kernel_name = 'mk_dlrm_tower_d1_rec_r8_0ed058'

def setup_inputs(seed: int=0):
    np.random.seed(seed)
    _w = jnp.asarray

    def _rec_inputs():
        import jax
        import jax.numpy as jnp
        _tk = jax.random.key(seed)
        dense_ctx = jax.random.normal(jax.random.fold_in(_tk, 190), (1024, 16), jnp.float32)
        ids = jnp.stack([jax.random.randint(jax.random.fold_in(_tk, 200 + f), (1024,), 0, v, jnp.int32) for f, v in enumerate([12500, 1000, 1250, 1000, 12500, 12500, 12500, 1000, 1000, 12500, 1250, 1250, 1000, 1000, 1000, 125000, 125000, 1000, 1250, 1000, 1000, 125000, 125000, 1250, 12500, 1000, 1000, 12500, 12500, 1250, 1250, 12500, 1250, 12500, 125000, 1250, 12500, 125000, 125000, 125000])], axis=1)
        tbl_0 = 0.05 * jax.random.normal(jax.random.fold_in(_tk, 500 + 0), (12500, 16), jnp.float32)
        tbl_1 = 0.05 * jax.random.normal(jax.random.fold_in(_tk, 500 + 1), (1000, 16), jnp.float32)
        tbl_2 = 0.05 * jax.random.normal(jax.random.fold_in(_tk, 500 + 2), (1250, 16), jnp.float32)
        tbl_3 = 0.05 * jax.random.normal(jax.random.fold_in(_tk, 500 + 3), (1000, 16), jnp.float32)
        tbl_4 = 0.05 * jax.random.normal(jax.random.fold_in(_tk, 500 + 4), (12500, 16), jnp.float32)
        tbl_5 = 0.05 * jax.random.normal(jax.random.fold_in(_tk, 500 + 5), (12500, 16), jnp.float32)
        tbl_6 = 0.05 * jax.random.normal(jax.random.fold_in(_tk, 500 + 6), (12500, 16), jnp.float32)
        tbl_7 = 0.05 * jax.random.normal(jax.random.fold_in(_tk, 500 + 7), (1000, 16), jnp.float32)
        tbl_8 = 0.05 * jax.random.normal(jax.random.fold_in(_tk, 500 + 8), (1000, 16), jnp.float32)
        tbl_9 = 0.05 * jax.random.normal(jax.random.fold_in(_tk, 500 + 9), (12500, 16), jnp.float32)
        tbl_10 = 0.05 * jax.random.normal(jax.random.fold_in(_tk, 500 + 10), (1250, 16), jnp.float32)
        tbl_11 = 0.05 * jax.random.normal(jax.random.fold_in(_tk, 500 + 11), (1250, 16), jnp.float32)
        tbl_12 = 0.05 * jax.random.normal(jax.random.fold_in(_tk, 500 + 12), (1000, 16), jnp.float32)
        tbl_13 = 0.05 * jax.random.normal(jax.random.fold_in(_tk, 500 + 13), (1000, 16), jnp.float32)
        tbl_14 = 0.05 * jax.random.normal(jax.random.fold_in(_tk, 500 + 14), (1000, 16), jnp.float32)
        tbl_15 = 0.05 * jax.random.normal(jax.random.fold_in(_tk, 500 + 15), (125000, 16), jnp.float32)
        tbl_16 = 0.05 * jax.random.normal(jax.random.fold_in(_tk, 500 + 16), (125000, 16), jnp.float32)
        tbl_17 = 0.05 * jax.random.normal(jax.random.fold_in(_tk, 500 + 17), (1000, 16), jnp.float32)
        tbl_18 = 0.05 * jax.random.normal(jax.random.fold_in(_tk, 500 + 18), (1250, 16), jnp.float32)
        tbl_19 = 0.05 * jax.random.normal(jax.random.fold_in(_tk, 500 + 19), (1000, 16), jnp.float32)
        tbl_20 = 0.05 * jax.random.normal(jax.random.fold_in(_tk, 500 + 20), (1000, 16), jnp.float32)
        tbl_21 = 0.05 * jax.random.normal(jax.random.fold_in(_tk, 500 + 21), (125000, 16), jnp.float32)
        tbl_22 = 0.05 * jax.random.normal(jax.random.fold_in(_tk, 500 + 22), (125000, 16), jnp.float32)
        tbl_23 = 0.05 * jax.random.normal(jax.random.fold_in(_tk, 500 + 23), (1250, 16), jnp.float32)
        tbl_24 = 0.05 * jax.random.normal(jax.random.fold_in(_tk, 500 + 24), (12500, 16), jnp.float32)
        tbl_25 = 0.05 * jax.random.normal(jax.random.fold_in(_tk, 500 + 25), (1000, 16), jnp.float32)
        tbl_26 = 0.05 * jax.random.normal(jax.random.fold_in(_tk, 500 + 26), (1000, 16), jnp.float32)
        tbl_27 = 0.05 * jax.random.normal(jax.random.fold_in(_tk, 500 + 27), (12500, 16), jnp.float32)
        tbl_28 = 0.05 * jax.random.normal(jax.random.fold_in(_tk, 500 + 28), (12500, 16), jnp.float32)
        tbl_29 = 0.05 * jax.random.normal(jax.random.fold_in(_tk, 500 + 29), (1250, 16), jnp.float32)
        tbl_30 = 0.05 * jax.random.normal(jax.random.fold_in(_tk, 500 + 30), (1250, 16), jnp.float32)
        tbl_31 = 0.05 * jax.random.normal(jax.random.fold_in(_tk, 500 + 31), (12500, 16), jnp.float32)
        tbl_32 = 0.05 * jax.random.normal(jax.random.fold_in(_tk, 500 + 32), (1250, 16), jnp.float32)
        tbl_33 = 0.05 * jax.random.normal(jax.random.fold_in(_tk, 500 + 33), (12500, 16), jnp.float32)
        tbl_34 = 0.05 * jax.random.normal(jax.random.fold_in(_tk, 500 + 34), (125000, 16), jnp.float32)
        tbl_35 = 0.05 * jax.random.normal(jax.random.fold_in(_tk, 500 + 35), (1250, 16), jnp.float32)
        tbl_36 = 0.05 * jax.random.normal(jax.random.fold_in(_tk, 500 + 36), (12500, 16), jnp.float32)
        tbl_37 = 0.05 * jax.random.normal(jax.random.fold_in(_tk, 500 + 37), (125000, 16), jnp.float32)
        tbl_38 = 0.05 * jax.random.normal(jax.random.fold_in(_tk, 500 + 38), (125000, 16), jnp.float32)
        tbl_39 = 0.05 * jax.random.normal(jax.random.fold_in(_tk, 500 + 39), (125000, 16), jnp.float32)
        _rk = jax.random.fold_in(_tk, 7)
        W_top1 = 0.05 * jax.random.normal(jax.random.fold_in(_tk, 801), (400, 512), jnp.float32)
        W_top2 = 0.0441942 * jax.random.normal(jax.random.fold_in(_tk, 802), (512, 256), jnp.float32)
        W_top3 = 0.0625 * jax.random.normal(jax.random.fold_in(_tk, 803), (256, 1), jnp.float32)
        b_top1 = jnp.zeros((512,), jnp.float32)
        b_top2 = jnp.zeros((256,), jnp.float32)
        return (dense_ctx, ids, tbl_0, tbl_1, tbl_2, tbl_3, tbl_4, tbl_5, tbl_6, tbl_7, tbl_8, tbl_9, tbl_10, tbl_11, tbl_12, tbl_13, tbl_14, tbl_15, tbl_16, tbl_17, tbl_18, tbl_19, tbl_20, tbl_21, tbl_22, tbl_23, tbl_24, tbl_25, tbl_26, tbl_27, tbl_28, tbl_29, tbl_30, tbl_31, tbl_32, tbl_33, tbl_34, tbl_35, tbl_36, tbl_37, tbl_38, tbl_39, W_top1, b_top1, W_top2, b_top2, W_top3)
    dense_ctx, ids, tbl_0, tbl_1, tbl_2, tbl_3, tbl_4, tbl_5, tbl_6, tbl_7, tbl_8, tbl_9, tbl_10, tbl_11, tbl_12, tbl_13, tbl_14, tbl_15, tbl_16, tbl_17, tbl_18, tbl_19, tbl_20, tbl_21, tbl_22, tbl_23, tbl_24, tbl_25, tbl_26, tbl_27, tbl_28, tbl_29, tbl_30, tbl_31, tbl_32, tbl_33, tbl_34, tbl_35, tbl_36, tbl_37, tbl_38, tbl_39, W_top1, b_top1, W_top2, b_top2, W_top3 = _rec_inputs()

    def _L0_rec_setup():
        import jax, jax.numpy as jnp
        import numpy as np
        B, M, D = (512, 40, 16)
        DIMS = [128, 128, 128]
        key = jax.random.key(seed)
        k_x, k0, k1, k2 = jax.random.split(key, 4)
        scale = lambda fan_in: (2.0 / fan_in) ** 0.5
        x0 = jax.random.normal(k_x, (B, M, D), dtype=jnp.float32)
        kern0 = jax.random.normal(k0, (DIMS[0], M, M), dtype=jnp.float32) * scale(M * M)
        kern1 = jax.random.normal(k1, (DIMS[1], DIMS[0], M), dtype=jnp.float32) * scale(DIMS[0] * M)
        kern2 = jax.random.normal(k2, (DIMS[2], DIMS[1], M), dtype=jnp.float32) * scale(DIMS[1] * M)
        return {'x0': x0, 'k0': kern0, 'k1': kern1, 'k2': kern2}
    _L0_rec_all = _L0_rec_setup()
    _L0_rec_in = {k: v for k, v in _L0_rec_all.items() if k in ('k0', 'k1', 'k2')}
    del _L0_rec_all
    return {'dense_ctx': dense_ctx, 'ids': ids, 'tbl_0': tbl_0, 'tbl_1': tbl_1, 'tbl_2': tbl_2, 'tbl_3': tbl_3, 'tbl_4': tbl_4, 'tbl_5': tbl_5, 'tbl_6': tbl_6, 'tbl_7': tbl_7, 'tbl_8': tbl_8, 'tbl_9': tbl_9, 'tbl_10': tbl_10, 'tbl_11': tbl_11, 'tbl_12': tbl_12, 'tbl_13': tbl_13, 'tbl_14': tbl_14, 'tbl_15': tbl_15, 'tbl_16': tbl_16, 'tbl_17': tbl_17, 'tbl_18': tbl_18, 'tbl_19': tbl_19, 'tbl_20': tbl_20, 'tbl_21': tbl_21, 'tbl_22': tbl_22, 'tbl_23': tbl_23, 'tbl_24': tbl_24, 'tbl_25': tbl_25, 'tbl_26': tbl_26, 'tbl_27': tbl_27, 'tbl_28': tbl_28, 'tbl_29': tbl_29, 'tbl_30': tbl_30, 'tbl_31': tbl_31, 'tbl_32': tbl_32, 'tbl_33': tbl_33, 'tbl_34': tbl_34, 'tbl_35': tbl_35, 'tbl_36': tbl_36, 'tbl_37': tbl_37, 'tbl_38': tbl_38, 'tbl_39': tbl_39, 'W_top1': W_top1, 'b_top1': b_top1, 'W_top2': W_top2, 'b_top2': b_top2, 'W_top3': W_top3, 'L0_rec_k0': _L0_rec_in['k0'], 'L0_rec_k1': _L0_rec_in['k1'], 'L0_rec_k2': _L0_rec_in['k2']}

def reference(dense_ctx, ids, tbl_0, tbl_1, tbl_2, tbl_3, tbl_4, tbl_5, tbl_6, tbl_7, tbl_8, tbl_9, tbl_10, tbl_11, tbl_12, tbl_13, tbl_14, tbl_15, tbl_16, tbl_17, tbl_18, tbl_19, tbl_20, tbl_21, tbl_22, tbl_23, tbl_24, tbl_25, tbl_26, tbl_27, tbl_28, tbl_29, tbl_30, tbl_31, tbl_32, tbl_33, tbl_34, tbl_35, tbl_36, tbl_37, tbl_38, tbl_39, W_top1, b_top1, W_top2, b_top2, W_top3, L0_rec_k0, L0_rec_k1, L0_rec_k2):
    import jax
    import jax.numpy as jnp

    def _L0_rec_ref(x0, k0, k1, k2):
        import jax, jax.numpy as jnp
        import numpy as np
        B, M, D = (512, 40, 16)
        DIMS = [128, 128, 128]
        x = x0
        outputs = []
        for k in (k0, k1, k2):
            x = jnp.einsum('bhd,bmd,ohm->bod', x, x0, k)
            outputs.append(jnp.sum(x, axis=-1))
        return jnp.concatenate(outputs, axis=1)
    e = jnp.stack([tbl_0[ids[:, 0]], tbl_1[ids[:, 1]], tbl_2[ids[:, 2]], tbl_3[ids[:, 3]], tbl_4[ids[:, 4]], tbl_5[ids[:, 5]], tbl_6[ids[:, 6]], tbl_7[ids[:, 7]], tbl_8[ids[:, 8]], tbl_9[ids[:, 9]], tbl_10[ids[:, 10]], tbl_11[ids[:, 11]], tbl_12[ids[:, 12]], tbl_13[ids[:, 13]], tbl_14[ids[:, 14]], tbl_15[ids[:, 15]], tbl_16[ids[:, 16]], tbl_17[ids[:, 17]], tbl_18[ids[:, 18]], tbl_19[ids[:, 19]], tbl_20[ids[:, 20]], tbl_21[ids[:, 21]], tbl_22[ids[:, 22]], tbl_23[ids[:, 23]], tbl_24[ids[:, 24]], tbl_25[ids[:, 25]], tbl_26[ids[:, 26]], tbl_27[ids[:, 27]], tbl_28[ids[:, 28]], tbl_29[ids[:, 29]], tbl_30[ids[:, 30]], tbl_31[ids[:, 31]], tbl_32[ids[:, 32]], tbl_33[ids[:, 33]], tbl_34[ids[:, 34]], tbl_35[ids[:, 35]], tbl_36[ids[:, 36]], tbl_37[ids[:, 37]], tbl_38[ids[:, 38]], tbl_39[ids[:, 39]]], axis=1)
    z = _L0_rec_ref(e, L0_rec_k0, L0_rec_k1, L0_rec_k2)
    z = z.reshape(z.shape[0], -1)
    h = jnp.concatenate([z, dense_ctx], axis=1)
    h = jnp.maximum(h @ W_top1 + b_top1, 0.0)
    h = jnp.maximum(h @ W_top2 + b_top2, 0.0)
    y = h @ W_top3
    return y

_drawn_inputs = setup_inputs


def setup_inputs(seed=0):
    import zlib

    import numpy as np

    out = dict(_drawn_inputs(seed))
    spreads = {'b_top1': (0.0, 0.477), 'b_top2': (0.0, 0.1)}
    factors = {'tbl_0': 7.401,
     'tbl_1': 6.876,
     'tbl_2': 6.725,
     'tbl_3': 6.996,
     'tbl_4': 7.091,
     'tbl_5': 7.02,
     'tbl_6': 6.775,
     'tbl_7': 7.19,
     'tbl_8': 6.546,
     'tbl_9': 7.028,
     'tbl_10': 6.78,
     'tbl_11': 6.674,
     'tbl_12': 6.609,
     'tbl_13': 6.889,
     'tbl_14': 6.731,
     'tbl_15': 6.642,
     'tbl_16': 7.074,
     'tbl_17': 6.113,
     'tbl_18': 7.138,
     'tbl_19': 6.417,
     'tbl_20': 7.133,
     'tbl_21': 7.536,
     'tbl_22': 6.821,
     'tbl_23': 6.374,
     'tbl_24': 7.202,
     'tbl_25': 6.592,
     'tbl_26': 6.708,
     'tbl_27': 6.666,
     'tbl_28': 6.458,
     'tbl_29': 7.025,
     'tbl_30': 6.984,
     'tbl_31': 7.003,
     'tbl_32': 6.871,
     'tbl_33': 6.056,
     'tbl_34': 6.781,
     'tbl_35': 6.09,
     'tbl_36': 6.464,
     'tbl_37': 6.421,
     'tbl_38': 7.087,
     'tbl_39': 6.064,
     'L0_rec_k1': 8.0,
     'L0_rec_k2': 8.0}
    for name, (base, spread) in spreads.items():
        noise = np.random.default_rng([zlib.crc32(name.encode()), seed]).standard_normal(out[name].shape)
        drawn = base * np.exp(spread * noise) if base else spread * noise
        out[name] = jnp.asarray(drawn.astype(out[name].dtype))
    for name, factor in factors.items():
        out[name] = (out[name] * factor).astype(out[name].dtype)
    return out
```

```python
from contextlib import ExitStack

import numpy as np

import concourse.bass as bass
from concourse import mybir

B, M, D, H = 1024, 40, 16, 128
TILE_B, GROUP_B, CHUNK_B = 128, 32, 8
TILES = B // TILE_B
GROUPS = TILE_B // GROUP_B
CHUNKS = GROUP_B // CHUNK_B
TILE_CHUNKS = GROUPS * CHUNKS
NG = GROUP_B * D
NC = CHUNK_B * D
BANK_M = 512 // H
STEPS = M // BANK_M
GSTEPS = STEPS * CHUNKS
HALF = STEPS // 2
STTS = HALF * BANK_M
LO = 64
EK = LO + M
REP = 3
PR = REP * M
BLOCKS = (M // 2 + 1) // REP
GM = M + 1
TABLES = M
PARTIALS = BANK_M + 2

CREDIT_STT = 2 * BANK_M
CREDIT_ACT = 2
CREDIT_ADD = 4
CREDIT_ONE = 1


def build(nc, ids, tables, ident_in, sel_in, mask_in, k0a_in, k0b_in, k1_in, k2_in, w1_in, w1d_in,
          b1_in, w2_in, b2_in, w3_in, dense_in, out):
    f32, f32r, i32 = mybir.dt.float32, mybir.dt.float32r, mybir.dt.int32
    ALU, ACT, AX = mybir.AluOpType, mybir.ActivationFunctionType, mybir.AxisListType
    ctx = ExitStack()
    with ctx:
        def sb(name, shape, dt=f32):
            return ctx.enter_context(nc.sbuf_tensor(name, shape, dt))

        def sem(name):
            return ctx.enter_context(nc.semaphore(name))

        idx = sb("idx", [TILE_B, M], i32)
        rows = sb("rows", [TILE_B, M, D])
        ident = sb("ident", [128, 128])
        sel_raw = sb("sel_raw", [EK, 8 * PR + M])
        sel = sb("sel", [EK, 8 * PR + M], f32r)
        mask = sb("mask", [128, CHUNK_B])
        w0H = sb("w0H", [PR, BLOCKS, H], f32r)
        w0L = sb("w0L", [PR, BLOCKS, H], f32r)
        k1H = sb("k1H", [H, M * H], f32r)
        k1L = sb("k1L", [H, M * H], f32r)
        k2 = sb("k2", [H, M, H])
        w1 = sb("w1", [H, 3, 512])
        w1d = sb("w1d", [D, 512])
        b1 = sb("b1", [128, 4])
        w2 = sb("w2", [128, 4, 256])
        b2 = sb("b2", [128, 2])
        w3 = sb("w3", [128, 2])
        dense = sb("dense", [D, B])
        eHL = sb("eHL", [EK, TILE_B, D], f32r)
        eT = sb("eT", [128, 2 * TILE_CHUNKS * M])
        eTc = sb("eTc", [128, 2, M])
        eRep = sb("eRep", [PR, NG])
        prod = sb("prod", [PR, 2, NG])
        prodH = sb("prodH", [PR, 2, NG], f32r)
        prodL = sb("prodL", [PR, 2, NG], f32r)
        xH = sb("xH", [H, NG], f32r)
        xL = sb("xL", [H, NG], f32r)
        scaled = sb("scaled", [128, 4, BANK_M * H])
        part = sb("part", [128, 2, PARTIALS, H])
        x2 = sb("x2", [128, 2, H])
        eBlk = sb("eBlk", [128, 2, CHUNK_B, GM])
        G = sb("G", [H, 2, GM, TILE_B])
        z1 = sb("z1", [H, B])
        z2 = sb("z2", [H, B])
        z3 = sb("z3", [H, B])
        y = sb("y", [1, B])
        Gflat = G[:, :, :, :].rearrange("p a m b -> p (a m b)")
        k1raw = Gflat[:, 0:M * H]
        w0a = Gflat[0:PR, M * H:M * H + BLOCKS * H]
        w0b = Gflat[0:PR, M * H + BLOCKS * H:M * H + 2 * BLOCKS * H]
        h1 = scaled
        h2 = sb("h2", [128, 2, 512])

        def bank(name):
            return ctx.enter_context(nc.psum_tensor(name, [128, 512], f32))

        Y = [bank(f"Y{i}") for i in range(4)]
        pSel, pZ, pX1, pG = bank("pSel"), bank("pZ"), bank("pX1"), bank("pG")

        idx_in, consts_in, w0_in, k1_loaded, tail_in = map(
            sem, ("idx_in", "consts_in", "w0_in", "k1_loaded", "tail_in"))
        gathered = sem("gathered")
        rows_used = sem("rows_used")
        sel_ready = sem("sel_ready")
        w0_sum = sem("w0_sum")
        w0_high = sem("w0_high")
        k_ready = sem("k_ready")
        prep_ps = sem("prep_ps")
        prep_high = sem("prep_high")
        prep_low = sem("prep_low")
        eT_ready = sem("eT_ready")
        rep_ps = sem("rep_ps")
        rep_ready = sem("rep_ready")
        shift_ps = sem("shift_ps")
        prod_ready = sem("prod_ready")
        prodH_ready = sem("prodH_ready")
        prodL_ready = sem("prodL_ready")
        prod_used = sem("prod_used")
        xH_ready = sem("xH_ready")
        xL_ready = sem("xL_ready")
        y_even = sem("y_even")
        y_odd = sem("y_odd")
        stt_done = sem("stt_done")
        act_done = sem("act_done")
        add_done = sem("add_done")
        x2_ready = sem("x2_ready")
        eTc_ready = sem("eTc_ready")
        eBlk_ready = sem("eBlk_ready")
        g_ps = sem("g_ps")
        g_copied = sem("g_copied")
        z3_ps = sem("z3_ps")
        z_copied = sem("z_copied")
        mask_set = sem("mask_set")
        mlp_ps = sem("mlp_ps")
        mlp_act = sem("mlp_act")
        stored = sem("stored")

        block = ctx.enter_context(nc.Block())

        def sel_m(q):
            return sel[:, q * PR:(q + 1) * PR]

        def eT_at(T, ch):
            return (T % 2) * (TILE_CHUNKS * M) + ch * M

        def layer1_times(prep):
            rep, first, gap = (13, 15, 3) if prep else (2, 4, 4)
            return rep, [first + gap * j for j in range(BLOCKS)]

        def in_steps(bank_work, others):
            for s in range(GSTEPS):
                for at, what in others:
                    if at == s:
                        what()
                bank_work(s)
            for at, what in others:
                if at >= GSTEPS:
                    what()

        def all_tiles(eng, tile):
            tile(0, True, False)
            with eng.Fori(1, TILES - 1) as t:
                tile(t, False, False)
            tile(TILES - 1, False, True)

        @block.sync
        def _(sp):
            sp.dma_start(idx[:, :], ids[0:TILE_B, :]).then_inc(idx_in, 16)
            sp.dma_start(ident[:, :], ident_in).then_inc(consts_in, 16)
            sp.dma_start(sel_raw[:, :], sel_in).then_inc(consts_in, 16)
            sp.dma_start(mask[:, :], mask_in).then_inc(consts_in, 16)
            sp.dma_start(w0a, k0a_in).then_inc(w0_in, 16)
            sp.dma_start(w0b, k0b_in).then_inc(w0_in, 16)
            sp.dma_start(k1raw, k1_in).then_inc(k1_loaded, 16)
            sp.dma_start(k2[:, :, :], k2_in).then_inc(tail_in, 16)
            sp.dma_start(w1[:, :, :], w1_in).then_inc(tail_in, 16)
            sp.dma_start(w1d[:, :], w1d_in).then_inc(tail_in, 16)
            sp.dma_start(b1[:, :], b1_in).then_inc(tail_in, 16)
            sp.dma_start(w2[:, :, :], w2_in).then_inc(tail_in, 16)
            sp.dma_start(b2[:, :], b2_in).then_inc(tail_in, 16)
            sp.dma_start(w3[:, :], w3_in).then_inc(tail_in, 16)
            sp.dma_start(dense[:, :], dense_in).then_inc(tail_in, 16)
            with sp.Fori(1, TILES) as t:
                sp.wait_ge(rows_used, t)
                sp.dma_start(idx[:, :], ids[bass.ds(t * TILE_B, TILE_B), :]).then_inc(idx_in, 16)
            sp.wait_ge(mlp_act, 14)
            sp.dma_start(out.rearrange("b one -> one b"), y[:, :]).then_inc(stored, 16)
            sp.wait_ge(stored, 16)

        @block.gpsimd
        def _(pool):
            pool.sem_inc(add_done, CREDIT_ADD)

            def gather(f):
                pool.indirect_dma_start(rows[:, f, :], None, tables[f],
                                        bass.IndirectOffsetOnAxis(idx[:, f:f + 1], 0)
                                        ).then_inc(gathered, 16)

            pool.wait_ge(idx_in, 16)
            for f in range(TABLES):
                gather(f)
            pool.wait_ge(consts_in, 48)
            for slot in range(2):
                pool.tensor_copy(eBlk[:, slot, :, M], mask[:, :]).then_inc(mask_set, 1)

            def scalars_of(C, T, ch, slot):
                pool.wait_ge(eT_ready, 2 * T + 2)
                pool.wait_ge(stt_done, STTS * (C - 1) + CREDIT_STT)
                pool.wait_ge(act_done, HALF * (C - 1) + CREDIT_ACT)
                at = eT_at(T, ch)
                pool.tensor_copy(eTc[:, slot, :], eT[:, bass.ds(at, M)]).then_inc(eTc_ready, 1)
                pool.wait_ge(eTc_ready, C + 1)
                pool.wait_ge(g_ps, C)
                pool.tensor_tensor(
                    eBlk[:, slot, :, 0:M], mask[:, :, None].to_broadcast([128, CHUNK_B, M]),
                    eTc[:, slot, None, :].to_broadcast([128, CHUNK_B, M]),
                    ALU.mult).then_inc(eBlk_ready, 1)

            def first_scalars():
                pool.wait_ge(eT_ready, 2)
                pool.tensor_copy(eTc[:, 0, :], eT[:, 0:M]).then_inc(eTc_ready, 1)
                pool.tensor_tensor(
                    eBlk[:, 0, :, 0:M], mask[:, :, None].to_broadcast([128, CHUNK_B, M]),
                    eT[:, None, 0:M].to_broadcast([128, CHUNK_B, M]), ALU.mult
                ).then_inc(eBlk_ready, 1)

            def tile(T, first, last):
                fields = list(range(TABLES))
                for ch in range(TILE_CHUNKS):
                    C = T * TILE_CHUNKS + ch
                    slot = ch % 2
                    acc = part[:, slot, 0:BANK_M, :].rearrange("p a h -> p (a h)")
                    if ch == 0 and not last:
                        pool.wait_ge(idx_in, 16 * (T + 2))
                    for i in range(1, HALF):
                        k = ch * HALF + i
                        pool.wait_ge(act_done, HALF * C + i + 1 + CREDIT_ACT)
                        if i == 1:
                            pool.wait_ge(x2_ready, C)
                            a, b_ = scaled[:, (k - 1) % 4, :], scaled[:, k % 4, :]
                        else:
                            pool.wait_ge(add_done, 4 * C + (i - 1) + CREDIT_ADD)
                            a, b_ = acc, scaled[:, k % 4, :]
                        pool.tensor_tensor(acc, a, b_, ALU.add).then_inc(add_done, 1)
                        if i == 2 and not (last and ch == TILE_CHUNKS - 1):
                            nxt = ch + 1
                            if nxt < TILE_CHUNKS:
                                scalars_of(C + 1, T, nxt, 1 - slot)
                            else:
                                scalars_of(C + 1, T + 1, 0, 1 - slot)
                        if not last and fields and (i != 2 or ch < CHUNKS):
                            gather(fields.pop(0))
                assert last or not fields

            first_scalars()
            all_tiles(pool, tile)

        @block.vector
        def _(dve):
            dve.sem_inc(stt_done, CREDIT_STT)
            dve.sem_inc(x2_ready, CREDIT_ONE)
            dve.memset(eHL[:, :, :].bitcast(f32), 0.0).then_inc(sel_ready, 1)
            dve.wait_ge(consts_in, 48)
            dve.tensor_copy(sel[:, :], sel_raw[:, :]).then_inc(sel_ready, 1)
            dve.wait_ge(w0_in, 32)
            dve.tensor_tensor(w0a, w0a, w0b, ALU.add).then_inc(w0_sum, 1)
            dve.wait_ge(w0_high, 1)
            dve.tensor_tensor(w0L[:, :, :].rearrange("p j h -> p (j h)"), w0a,
                              w0H[:, :, :].rearrange("p j h -> p (j h)").bitcast(f32),
                              ALU.subtract).then_inc(k_ready, 1)
            dve.wait_ge(w0_high, 2)
            dve.tensor_tensor(k1L[:, :], k1raw, k1H[:, :].bitcast(f32),
                              ALU.subtract).then_inc(k_ready, 1)

            def prep_l(T, r):
                dve.wait_ge(prep_high, 4 * T + r + 1)
                src = (pSel if r % 2 == 0 else pZ)[0:M, :].rearrange("m (d b) -> m b d", d=4)
                dve.tensor_tensor(eHL[LO:EK, :, 4 * r:4 * r + 4], src,
                                  eHL[0:M, :, 4 * r:4 * r + 4].bitcast(f32),
                                  ALU.subtract).then_inc(prep_low, 1)

            def product(S, j):
                dve.wait_ge(shift_ps, BLOCKS * S + j + 1)
                if j == 0:
                    dve.wait_ge(rep_ready, S + 1)
                used = BLOCKS * S + max(j - 1, 0)
                dve.wait_ge(prodH_ready, used)
                dve.wait_ge(prodL_ready, used)
                dve.tensor_tensor(prod[:, j % 2, :], pSel[0:PR, :], eRep[:, :],
                                  ALU.mult).then_inc(prod_ready, 1)

            def product_l(S, j):
                dve.wait_ge(prodH_ready, BLOCKS * S + j + 1)
                dve.wait_ge(prod_used, BLOCKS * S + max(j - 1, 0))
                dve.tensor_tensor(prodL[:, j % 2, :], prod[:, j % 2, :],
                                  prodH[:, j % 2, :].bitcast(f32),
                                  ALU.subtract).then_inc(prodL_ready, 1)

            def x_low(S, part_):
                lo, hi = ((0, 3 * NC), (3 * NC, NG))[part_]
                dve.wait_ge(xH_ready, 2 * S + part_ + 1)
                if part_:
                    dve.tensor_reduce(z1[:, bass.ds(S * GROUP_B, GROUP_B)],
                                      pX1[:, :].rearrange("h (b d) -> h b d", d=D),
                                      AX.X, ALU.add)
                dve.tensor_tensor(xL[:, lo:hi], pX1[:, lo:hi], xH[:, lo:hi].bitcast(f32),
                                  ALU.subtract).then_inc(xL_ready, 1)

            def sum_x2(C, slot):
                dve.wait_ge(add_done, 4 * C + 4 + CREDIT_ADD)
                dve.wait_ge(stt_done, STTS * (C + 1) + CREDIT_STT)
                dve.wait_ge(g_ps, C)
                dve.tensor_reduce(x2[:, slot, :], part[:, slot, :, :].rearrange("p a h -> p h a"),
                                  AX.X, ALU.add).then_inc(x2_ready, 1)

            def group(T, g, nxt, prep, first):
                S = T * GROUPS + g

                def bank_work(s):
                    if s % 2:
                        return
                    c, i = divmod(s, STEPS)
                    C = S * CHUNKS + c
                    if i == 0:
                        dve.wait_ge(eTc_ready, C + 1)
                        dve.wait_ge(x2_ready, C)
                    dve.wait_ge(y_even, S * (GSTEPS // 2) + s // 2 + 1)
                    for q in range(BANK_M):
                        u = (i // 2) * BANK_M + q
                        scalar = eTc[:, c % 2, i * BANK_M + q:i * BANK_M + q + 1]
                        y_q = Y[s % 4][:, q * H:(q + 1) * H]
                        acc = part[:, c % 2, BANK_M + u % 2, :]
                        if u < 2:
                            dve.tensor_scalar(acc, y_q, scalar, None,
                                              ALU.mult).then_inc(stt_done, 1)
                        else:
                            dve.wait_ge(stt_done, STTS * C + u - 1 + CREDIT_STT)
                            dve.scalar_tensor_tensor(acc, y_q, scalar, acc, ALU.mult,
                                                     ALU.add).then_inc(stt_done, 1)

                others = [(3, lambda: x_low(S, 1))]
                for c in range(CHUNKS):
                    if not (first and c == 0):
                        others.append((c * STEPS + 7, lambda c=c: sum_x2(
                            S * CHUNKS + c - 1, (c + 1) % 2)))
                if prep:
                    for r, at in enumerate((3, 4, 7, 8)):
                        others.append((at, lambda r=r: prep_l(T + 1, r)))
                if nxt:
                    _, times = layer1_times(prep)
                    for j, at in enumerate(times):
                        others.append((at + 1, lambda j=j: product(S + 1, j)))
                        others.append((at + 3, lambda j=j: product_l(S + 1, j)))
                    others.append((max(times[-1] + 7, 37), lambda: x_low(S + 1, 0)))
                in_steps(bank_work, others)

            def tile(T, first, last):
                for g in range(GROUPS):
                    end = g == GROUPS - 1
                    group(T, g, not (last and end), end and not last, first and g == 0)

            for r in range(4):
                prep_l(0, r)
            for j in range(BLOCKS + 1):
                if j < BLOCKS:
                    product(0, j)
                if j:
                    product_l(0, j - 1)
            x_low(0, 0)
            all_tiles(dve, tile)
            sum_x2(TILES * TILE_CHUNKS - 1, 1)

        @block.scalar
        def _(act):
            act.sem_inc(act_done, CREDIT_ACT)
            act.preload_act_table(ACT.Relu)
            act.wait_ge(w0_sum, 1)
            act.activation(w0H[:, :, :].rearrange("p j h -> p (j h)"), w0a,
                           ACT.Copy).then_inc(w0_high, 1)
            act.wait_ge(k1_loaded, 16)
            act.activation(k1H[:, :], k1raw, ACT.Copy).then_inc(w0_high, 1)

            def prep_h(T, r):
                act.wait_ge(prep_ps, 6 * T + r + 1)
                if isinstance(T, int) and T == 0:
                    act.wait_ge(sel_ready, 1)
                src = (pSel if r % 2 == 0 else pZ)[0:M, :].rearrange("m (d b) -> m b d", d=4)
                act.activation(eHL[0:M, :, 4 * r:4 * r + 4], src, ACT.Copy).then_inc(prep_high, 1)

            def prep_eT(T, r):
                act.wait_ge(prep_ps, 6 * T + 4 + r + 1)
                n = TILE_CHUNKS * M // 2
                act.activation(eT[:, bass.ds(eT_at(T, 0) + r * n, n)],
                               (pSel if r == 0 else pZ)[:, 0:n], ACT.Copy).then_inc(eT_ready, 1)

            def rep(S):
                act.wait_ge(rep_ps, S + 1)
                act.activation(eRep[:, :], pSel[0:PR, :], ACT.Copy).then_inc(rep_ready, 1)

            def product_h(S, j):
                act.wait_ge(prod_ready, BLOCKS * S + j + 1)
                act.wait_ge(prod_used, BLOCKS * S + max(j - 1, 0))
                act.activation(prodH[:, j % 2, :], prod[:, j % 2, :],
                               ACT.Copy).then_inc(prodH_ready, 1)

            def x_high(S, part_):
                lo, hi = ((0, 3 * NC), (3 * NC, NG))[part_]
                act.wait_ge(prod_used, BLOCKS * (S + 1))
                act.activation(xH[:, lo:hi], pX1[:, lo:hi], ACT.Copy).then_inc(xH_ready, 1)

            def copy_G(C, T, ch):
                act.wait_ge(g_ps, C + 1 + CREDIT_ONE)
                dst = G[:, bass.ds(T % 2, 1), :, ch * CHUNK_B:(ch + 1) * CHUNK_B]
                act.activation(dst.rearrange("h one m b -> h (one b) m"),
                               pG[:, 0:CHUNK_B * GM].rearrange("h (b m) -> h b m", m=GM),
                               ACT.Copy).then_inc(g_copied, 1)

            def copy_z2(T):
                act.wait_ge(g_copied, TILE_CHUNKS * (T + 1))
                act.activation(z2[:, bass.ds(T * TILE_B, TILE_B)],
                               G[:, bass.ds(T % 2, 1), M, :].rearrange("h one b -> h (one b)"),
                               ACT.Copy)

            def copy_z3(T):
                act.wait_ge(z3_ps, T + 1)
                act.activation(z3[:, bass.ds(T * TILE_B, TILE_B)], pZ[:, 0:TILE_B],
                               ACT.Copy).then_inc(z_copied, 1)

            def group(T, g, nxt, prep, first):
                S = T * GROUPS + g

                def bank_work(s):
                    if s % 2 == 0:
                        return
                    c, i = divmod(s, STEPS)
                    C = S * CHUNKS + c
                    k = s // 2
                    if i == 1:
                        act.wait_ge(eTc_ready, C + 1)
                    act.wait_ge(add_done, 4 * C + i // 2 + 1)
                    act.wait_ge(y_odd, S * (GSTEPS // 2) + k + 1)
                    for q in range(BANK_M):
                        a = act.activation(scaled[:, k % 4, q * H:(q + 1) * H],
                                           Y[s % 4][:, q * H:(q + 1) * H], ACT.Copy,
                                           scale=eTc[:, c % 2, i * BANK_M + q:i * BANK_M + q + 1])
                    a.then_inc(act_done, 1)

                others = [(2, lambda: x_high(S, 1))]
                for c in range(CHUNKS):
                    if not (first and c == 0):
                        ch = g * CHUNKS + c - 1
                        others.append((c * STEPS + 10, lambda c=c, ch=ch: copy_G(
                            S * CHUNKS + c - 1, T if ch >= 0 else T - 1, ch % TILE_CHUNKS)))
                if g == 0 and not first:
                    others.append((12, lambda: copy_z2(T - 1)))
                    others.append((34, lambda: copy_z3(T - 1)))
                if prep:
                    for r, at in enumerate((2, 3, 6, 7)):
                        others.append((at, lambda r=r: prep_h(T + 1, r)))
                    others.append((12, lambda: prep_eT(T + 1, 0)))
                    others.append((13, lambda: prep_eT(T + 1, 1)))
                if nxt:
                    at_rep, times = layer1_times(prep)
                    others.append((at_rep + 1, lambda: rep(S + 1)))
                    for j, at in enumerate(times):
                        others.append((at + 2, lambda j=j: product_h(S + 1, j)))
                    others.append((max(times[-1] + 6, 36), lambda: x_high(S + 1, 0)))
                in_steps(bank_work, others)

            def tile(T, first, last):
                for g in range(GROUPS):
                    end = g == GROUPS - 1
                    group(T, g, not (last and end), end and not last, first and g == 0)

            for r in range(4):
                prep_h(0, r)
            prep_eT(0, 0)
            prep_eT(0, 1)
            rep(0)
            for j in range(BLOCKS):
                product_h(0, j)
            x_high(0, 0)
            all_tiles(act, tile)
            copy_G(TILES * TILE_CHUNKS - 1, TILES - 1, TILE_CHUNKS - 1)
            copy_z2(TILES - 1)
            copy_z3(TILES - 1)

            act.wait_ge(tail_in, 128)
            n = 0
            banks = [Y[0], Y[1], Y[2], Y[3]]
            for half in range(2):
                for o in range(4):
                    n += 1
                    act.wait_ge(mlp_ps, n)
                    act.activation(h1[:, o, :], banks[(n - 1) % 4][:, :], ACT.Relu,
                                   bias=b1[:, o:o + 1]).then_inc(mlp_act, 1)
                for o in range(2):
                    n += 1
                    act.wait_ge(mlp_ps, n)
                    act.activation(h2[:, o, :], banks[(n - 1) % 4][:, :], ACT.Relu,
                                   bias=b2[:, o:o + 1]).then_inc(mlp_act, 1)
                n += 1
                act.wait_ge(mlp_ps, n)
                act.activation(y[:, half * 512:(half + 1) * 512], banks[(n - 1) % 4][0:1, :],
                               ACT.Copy).then_inc(mlp_act, 1)

        @block.tensor
        def _(pe):
            pe.sem_inc(g_ps, CREDIT_ONE)

            def prep(T, r):
                ps = pSel if r % 2 == 0 else pZ
                if r == 0:
                    pe.wait_ge(gathered, 16 * TABLES * (T + 1))
                    pe.wait_ge(prod_ready, BLOCKS * GROUPS * T)
                elif r == 1:
                    if not (isinstance(T, int) and T == 0):
                        pe.wait_ge(z_copied, T - 1)
                else:
                    pe.wait_ge(prep_low, 4 * T + min(r, 5) - 1 + (r == 4))
                if r < 4:
                    for q in range(4):
                        a = pe.matmul(ps[0:M, q * TILE_B:(q + 1) * TILE_B], rows[:, :, 4 * r + q],
                                      ident[:, :], start=True, stop=True)
                    a.then_inc(prep_ps, 1)
                    if r == 3:
                        pe.wait_ge(prep_ps, 6 * T + 4)
                        pe.sem_inc(rows_used, 1)
                else:
                    for q in range(TILE_CHUNKS // 2):
                        c = (r - 4) * (TILE_CHUNKS // 2) + q
                        a = pe.matmul(ps[:, q * M:(q + 1) * M],
                                      eHL[:, c * CHUNK_B:(c + 1) * CHUNK_B, :].rearrange(
                                          "k b d -> k (b d)"),
                                      sel[:, 8 * PR:8 * PR + M], start=True, stop=True)
                    a.then_inc(prep_ps, 1)

            def e_group(g):
                return eHL[:, g * GROUP_B:(g + 1) * GROUP_B, :].rearrange("k b d -> k (b d)")

            def replicate(S, g, prepT):
                if prepT is not None:
                    pe.wait_ge(eT_ready, 2 * prepT + 1)
                else:
                    pe.wait_ge(prod_ready, BLOCKS * S)
                pe.matmul(pSel[0:PR, :], sel_m(0), e_group(g), start=True,
                          stop=True).then_inc(rep_ps, 1)

            def shift(S, g, j):
                if j == 0:
                    pe.wait_ge(rep_ready, S + 1)
                else:
                    pe.wait_ge(prod_ready, BLOCKS * S + j)
                pe.matmul(pSel[0:PR, :], sel_m(1 + j), e_group(g), start=True,
                          stop=True).then_inc(shift_ps, 1)

            def add_block(S, j):
                pe.wait_ge(prodL_ready, BLOCKS * S + j + 1)
                if j == 0:
                    pe.wait_ge(xL_ready, 2 * S)
                pe.matmul(pX1[:, :], w0H[:, j, :], prodH[:, j % 2, :], start=j == 0, stop=False)
                pe.matmul(pX1[:, :], w0L[:, j, :], prodH[:, j % 2, :], start=False, stop=False)
                pe.matmul(pX1[:, :], w0H[:, j, :], prodL[:, j % 2, :], start=False,
                          stop=j == BLOCKS - 1).then_inc(prod_used, 1)

            def make_G(C, slot):
                pe.wait_ge(x2_ready, C + 1 + CREDIT_ONE)
                pe.wait_ge(eBlk_ready, C + 1)
                pe.wait_ge(g_copied, C)
                pe.matmul(pG[:, 0:CHUNK_B * GM], x2[:, slot, :],
                          eBlk[:, slot, :, :].rearrange("n b m -> n (b m)"), start=True,
                          stop=True).then_inc(g_ps, 1)

            def z3_part(T, m0, m1):
                if m0 == 0:
                    pe.wait_ge(g_copied, TILE_CHUNKS * (T + 1))
                for m in range(m0, m1):
                    a = pe.matmul(pZ[:, 0:TILE_B], k2[:, m, :],
                                  G[:, bass.ds(T % 2, 1), m, :].rearrange("h one b -> h (one b)"),
                                  start=m == 0, stop=m == M - 1)
                if m1 == M:
                    a.then_inc(z3_ps, 1)

            def group(T, g, nxt, prep_next, first):
                S = T * GROUPS + g

                def bank_work(s):
                    c, i = divmod(s, STEPS)
                    k = S * (GSTEPS // 2) + s // 2
                    if s == 0:
                        pe.wait_ge(xL_ready, 2 * S + 1)
                    if s == 3 * STEPS:
                        pe.wait_ge(xL_ready, 2 * S + 2)
                    if s % 2 == 0:
                        pe.wait_ge(stt_done, BANK_M * (k + 1) + BANK_M)
                    else:
                        pe.wait_ge(act_done, k + 1)
                    x, w = slice(c * NC, (c + 1) * NC), slice(i * 512, (i + 1) * 512)
                    pe.matmul(Y[s % 4][:, :], xH[:, x], k1H[:, w], start=True, stop=False)
                    pe.matmul(Y[s % 4][:, :], xH[:, x], k1L[:, w], start=False, stop=False)
                    pe.matmul(Y[s % 4][:, :], xL[:, x], k1H[:, w], start=False,
                              stop=True).then_inc(y_odd if s % 2 else y_even, 1)

                others = []
                for c in range(CHUNKS):
                    if not (first and c == 0):
                        others.append((c * STEPS + 9, lambda c=c: make_G(
                            S * CHUNKS + c - 1, (c + 1) % 2)))
                if g == 0 and not first:
                    for q in range(M // 2):
                        others.append((12 + q, lambda q=q: z3_part(T - 1, 2 * q, 2 * q + 2)))
                if prep_next:
                    for r, at in enumerate((0, 1, 4, 5, 10, 11)):
                        others.append((at, lambda r=r: prep(T + 1, r)))
                if nxt:
                    at_rep, times = layer1_times(prep_next)
                    gn = (g + 1) % GROUPS
                    others.append((at_rep, lambda: replicate(
                        S + 1, gn, T + 1 if prep_next else None)))
                    for j, at in enumerate(times):
                        others.append((at, lambda j=j: shift(S + 1, gn, j)))
                        others.append((at + 5, lambda j=j: add_block(S + 1, j)))
                in_steps(bank_work, others)

            def tile(T, first, last):
                for g in range(GROUPS):
                    end = g == GROUPS - 1
                    group(T, g, not (last and end), end and not last, first and g == 0)

            pe.wait_ge(consts_in, 48)
            for r in range(6):
                if r == 4:
                    pe.wait_ge(sel_ready, 2)
                prep(0, r)
            replicate(0, 0, 0)
            for j in range(BLOCKS + 1):
                if j < BLOCKS:
                    shift(0, 0, j)
                if j == 1:
                    pe.wait_ge(k_ready, 1)
                if j:
                    add_block(0, j - 1)
            pe.wait_ge(k_ready, 2)
            all_tiles(pe, tile)
            make_G(TILES * TILE_CHUNKS - 1, 1)
            pe.wait_ge(tail_in, 128)
            z3_part(TILES - 1, 0, M)

            pe.wait_ge(z_copied, TILES)
            pe.wait_ge(stt_done, STTS * TILES * TILE_CHUNKS + CREDIT_STT)
            pe.wait_ge(act_done, HALF * TILES * TILE_CHUNKS + CREDIT_ACT)
            n = 0
            for half in range(2):
                b = slice(half * 512, (half + 1) * 512)
                done = 7 * half
                for o in range(4):
                    oc = slice(o * 128, (o + 1) * 128)
                    ps = Y[n % 4]
                    if n >= 4:
                        pe.wait_ge(mlp_act, n - 3)
                    pe.matmul(ps[:, :], w1[:, 0, oc], z1[:, b], start=True, stop=False)
                    pe.matmul(ps[:, :], w1[:, 1, oc], z2[:, b], start=False, stop=False)
                    pe.matmul(ps[:, :], w1[:, 2, oc], z3[:, b], start=False, stop=False)
                    pe.matmul(ps[:, :], w1d[:, oc], dense[:, b], start=False,
                              stop=True).then_inc(mlp_ps, 1)
                    n += 1
                for o in range(2):
                    pe.wait_ge(mlp_act, done + 4)
                    for k in range(4):
                        a = pe.matmul(Y[n % 4][:, :], w2[:, k, o * 128:(o + 1) * 128],
                                      h1[:, k, :], start=k == 0, stop=k == 3)
                    a.then_inc(mlp_ps, 1)
                    n += 1
                pe.wait_ge(mlp_act, done + 6)
                for k in range(2):
                    a = pe.matmul(Y[n % 4][0:1, :], w3[:, k:k + 1], h2[:, k, :],
                                  start=k == 0, stop=k == 1)
                a.then_inc(mlp_ps, 1)
                n += 1


def _constants():
    sel = np.zeros((EK, 8 * PR + M), np.float32)
    for q in range(8):
        for r in range(REP):
            shift = 0 if q == 0 else REP * (q - 1) + r
            for a in range(M):
                for base in (0, LO):
                    sel[base + (a + shift) % M, q * PR + r * M + a] = 1.0
    for m in range(M):
        sel[m, 8 * PR + m] = sel[LO + m, 8 * PR + m] = 1.0
    mask = (np.arange(128)[:, None] // D == np.arange(CHUNK_B)[None, :]).astype(np.float32)
    return np.eye(128, dtype=np.float32), sel, mask


def kernel(**inputs):
    import concourse.bacc as bacc
    from concourse.bass_utils import run_bass_kernel_spmd

    x = {k: np.asarray(v) for k, v in inputs.items()}
    ident, sel, mask = _constants()
    k0 = x["L0_rec_k0"]
    a = np.arange(M)
    k0a = np.zeros((BLOCKS, REP, M, H), np.float32)
    k0b = np.zeros((BLOCKS, REP, M, H), np.float32)
    for s in range(BLOCKS * REP):
        k0a[s // REP, s % REP] = k0[:, a, (a + s) % M].T
        if 0 < s < M // 2:
            k0b[s // REP, s % REP] = k0[:, (a + s) % M, a].T

    def by_row(k):
        return np.ascontiguousarray(k.transpose(1, 2, 0, 3).reshape(PR, BLOCKS * H))

    arrays = {
        "ids": x["ids"],
        **{f"tbl_{f}": x[f"tbl_{f}"] for f in range(TABLES)},
        "ident": ident, "sel": sel, "mask": mask,
        "k0a": by_row(k0a), "k0b": by_row(k0b),
        "k1": x["L0_rec_k1"].transpose(1, 2, 0).reshape(H, M * H),
        "k2": x["L0_rec_k2"].transpose(1, 2, 0),
        "w1": x["W_top1"][0:3 * H].reshape(3, H, 512).transpose(1, 0, 2),
        "w1d": x["W_top1"][3 * H:],
        "b1": x["b_top1"].reshape(4, 128).T,
        "w2": x["W_top2"].reshape(4, 128, 256).transpose(1, 0, 2),
        "b2": x["b_top2"].reshape(2, 128).T,
        "w3": x["W_top3"].reshape(2, 128).T,
        "dense": x["dense_ctx"].T,
    }
    arrays = {f"in_{k}": np.ascontiguousarray(v) for k, v in arrays.items()}
    nc = bacc.Bacc("TRN2", target_bir_lowering=False, num_devices=1)
    aps = {k: nc.dram_tensor(k, v.shape, mybir.dt.from_np(v.dtype), kind="ExternalInput").ap()
           for k, v in arrays.items()}
    out = nc.dram_tensor("out", (B, 1), mybir.dt.float32, kind="ExternalOutput").ap()
    names = ("ident", "sel", "mask", "k0a", "k0b", "k1", "k2", "w1", "w1d", "b1", "w2", "b2",
             "w3", "dense")
    build(nc, aps["in_ids"], [aps[f"in_tbl_{f}"] for f in range(TABLES)],
          *[aps[f"in_{k}"] for k in names], out)
    r = run_bass_kernel_spmd(nc, [arrays], core_ids=[0])
    return r.results[0]["out"]
```

```python
from contextlib import ExitStack

import numpy as np

import concourse.bass as bass
from concourse import mybir

B, M, D, H = 1024, 40, 16, 128
TILE_B, GROUP_B, CHUNK_B = 128, 32, 8
TILES = B // TILE_B
GROUPS = TILE_B // GROUP_B
CHUNKS = GROUP_B // CHUNK_B
TILE_CHUNKS = GROUPS * CHUNKS
NG = GROUP_B * D
NC = CHUNK_B * D
BANK_M = 512 // H
STEPS = M // BANK_M
GSTEPS = STEPS * CHUNKS
DVE_STEPS = (0, 3, 5, 8)
ACT_STEPS = (1, 2, 4, 6, 7, 9)
NDVE, NACT = len(DVE_STEPS), len(ACT_STEPS)
STTS = NDVE * BANK_M
ADDS = NACT - 1
RING = 4
LO = 64
EK = LO + M
REP = 3
PR = REP * M
BLOCKS = (M // 2 + 1) // REP
GM = M + 1
TABLES = M
PARTIALS = BANK_M + 2

CREDIT_STT = 2 * BANK_M
CREDIT_ACT = 2
CREDIT_ADD = 3
CREDIT_ONE = 1


def build(nc, ids, tables, ident_in, sel_in, mask_in, k0a_in, k0b_in, k1_in, k2_in, w1_in, w1d_in,
          b1_in, w2_in, b2_in, w3_in, dense_in, out):
    f32, f32r, i32 = mybir.dt.float32, mybir.dt.float32r, mybir.dt.int32
    ALU, ACT, AX = mybir.AluOpType, mybir.ActivationFunctionType, mybir.AxisListType
    ctx = ExitStack()
    with ctx:
        def sb(name, shape, dt=f32):
            return ctx.enter_context(nc.sbuf_tensor(name, shape, dt))

        def sem(name):
            return ctx.enter_context(nc.semaphore(name))

        idx = sb("idx", [TILE_B, M], i32)
        rows = sb("rows", [TILE_B, M, D])
        ident = sb("ident", [128, 128])
        sel = sb("sel", [EK, 8 * PR + M], f32r)
        mask = sb("mask", [128, CHUNK_B])
        w0H = sb("w0H", [PR, BLOCKS, H], f32r)
        w0L = sb("w0L", [PR, BLOCKS, H], f32r)
        k1H = sb("k1H", [H, M * H], f32r)
        k1L = sb("k1L", [H, M * H], f32r)
        k2 = sb("k2", [H, M, H])
        w1 = sb("w1", [H, 3, 512])
        w1d = sb("w1d", [D, 512])
        b1 = sb("b1", [128, 4])
        w2 = sb("w2", [128, 4, 256])
        b2 = sb("b2", [128, 2])
        w3 = sb("w3", [128, 2])
        dense = sb("dense", [D, B])
        eHL = sb("eHL", [EK, TILE_B, D], f32r)
        eT = sb("eT", [128, TILE_CHUNKS, M])
        eTg = sb("eTg", [128, 2, CHUNKS, M])
        eRep = sb("eRep", [PR, NG])
        prod = sb("prod", [PR, 2, NG])
        prodH = sb("prodH", [PR, 2, NG], f32r)
        prodL = sb("prodL", [PR, 2, NG], f32r)
        xH = sb("xH", [H, NG], f32r)
        xL = sb("xL", [H, NG], f32r)
        scaled = sb("scaled", [128, 4, BANK_M * H])
        part = sb("part", [128, 2, PARTIALS, H])
        x2 = sb("x2", [128, 2, H])
        eBlk = sb("eBlk", [128, 2, CHUNKS, CHUNK_B, GM])
        G = sb("G", [H, 2, GM, TILE_B])
        z1 = sb("z1", [H, B])
        z2 = sb("z2", [H, B])
        z3 = sb("z3", [H, B])
        z3p = sb("z3p", [H, 3, TILE_B])
        y = sb("y", [1, B])
        Gflat = G[:, :, :, :].rearrange("p a m b -> p (a m b)")
        k1raw = Gflat[:, 0:M * H]
        w0a = Gflat[0:PR, M * H:M * H + BLOCKS * H]
        w0b = Gflat[0:PR, M * H + BLOCKS * H:M * H + 2 * BLOCKS * H]
        sel_raw = Gflat[0:EK, M * H + 2 * BLOCKS * H:M * H + 2 * BLOCKS * H + 8 * PR + M]
        h1 = scaled
        h2 = part[:, :, :, :].rearrange("p s a h -> p (s a h)")[:, 0:2 * 512].rearrange(
            "p (c n) -> p c n", c=2)

        def bank(name):
            return ctx.enter_context(nc.psum_tensor(name, [128, 512], f32))

        Y = [bank(f"Y{i}") for i in range(RING)]
        pSel = [bank("pSel0"), bank("pSel1")]
        pX1, pG = bank("pX1"), bank("pG")

        idx_in, consts_in, w0_in, k1_loaded, tail_in = map(
            sem, ("idx_in", "consts_in", "w0_in", "k1_loaded", "tail_in"))
        gathered = sem("gathered")
        rows_used = sem("rows_used")
        sel_ready = sem("sel_ready")
        w0_sum = sem("w0_sum")
        w0_high = sem("w0_high")
        k_ready = sem("k_ready")
        prep_ps = sem("prep_ps")
        prep_high = sem("prep_high")
        prep_low = sem("prep_low")
        eT_ready = sem("eT_ready")
        rep_ps = sem("rep_ps")
        rep_ready = sem("rep_ready")
        shift_ps = sem("shift_ps")
        prod_ready = sem("prod_ready")
        prodH_ready = sem("prodH_ready")
        prodL_ready = sem("prodL_ready")
        prod_used = sem("prod_used")
        xH_ready = sem("xH_ready")
        xL_ready = sem("xL_ready")
        y_dve = sem("y_dve")
        y_act = sem("y_act")
        stt_done = sem("stt_done")
        act_done = sem("act_done")
        add_done = sem("add_done")
        x2_ready = sem("x2_ready")
        eTg_in = [sem("eTg_in0"), sem("eTg_in1")]
        eBlk_in = [sem("eBlk_in0"), sem("eBlk_in1")]
        g_ps = sem("g_ps")
        g_copied = sem("g_copied")
        z3_ps = sem("z3_ps")
        z3_copied = sem("z3_copied")
        z3_ready = sem("z3_ready")
        z2_ready = sem("z2_ready")
        blk_clear = sem("blk_clear")
        mlp_ps = sem("mlp_ps")
        mlp_act = sem("mlp_act")
        stored = sem("stored")

        block = ctx.enter_context(nc.Block())

        def sel_m(q):
            return sel[:, q * PR:(q + 1) * PR]

        SHIFT_AT = [2 + 7 * j // 2 for j in range(BLOCKS)]
        PRODUCT, HIGH, LOW, ADD = 3, 5, 6, 10
        PREP_AT = (28, 29, 32, 33, 37, 38)
        Z3_AT = ((0, 24), (0, 34), (1, 4))
        Z3_M = (0, 13, 26, M)

        def wait_bank_free(pe, S, s):
            c, i = divmod(s - RING, STEPS)
            C = S * CHUNKS + c
            if i in DVE_STEPS:
                pe.wait_ge(stt_done, BANK_M * (NDVE * C + DVE_STEPS.index(i) + 1) + CREDIT_STT)
            else:
                pe.wait_ge(act_done, NACT * C + ACT_STEPS.index(i) + 1 + CREDIT_ACT)

        def group_count(T, g):
            return T * (GROUPS // 2) + g // 2 + 1

        def in_steps(bank_work, others):
            for s in range(GSTEPS):
                for at, what in others:
                    if at == s:
                        what()
                bank_work(s)
            for at, what in others:
                if at >= GSTEPS:
                    what()

        def all_tiles(eng, tile):
            tile(0, True, False)
            with eng.Fori(1, TILES - 1) as t:
                tile(t, False, False)
            tile(TILES - 1, False, True)

        @block.sync
        def _(sp):
            sp.dma_start(idx[:, :], ids[0:TILE_B, :]).then_inc(idx_in, 16)
            sp.dma_start(ident[:, :], ident_in).then_inc(consts_in, 16)
            sp.dma_start(sel_raw[:, :], sel_in).then_inc(consts_in, 16)
            sp.dma_start(mask[:, :], mask_in).then_inc(consts_in, 16)
            sp.dma_start(w0a, k0a_in).then_inc(w0_in, 16)
            sp.dma_start(w0b, k0b_in).then_inc(w0_in, 16)
            sp.dma_start(k1raw, k1_in).then_inc(k1_loaded, 16)
            sp.dma_start(k2[:, :, :], k2_in).then_inc(tail_in, 16)
            sp.dma_start(w1[:, :, :], w1_in).then_inc(tail_in, 16)
            sp.dma_start(w1d[:, :], w1d_in).then_inc(tail_in, 16)
            sp.dma_start(b1[:, :], b1_in).then_inc(tail_in, 16)
            sp.dma_start(w2[:, :, :], w2_in).then_inc(tail_in, 16)
            sp.dma_start(b2[:, :], b2_in).then_inc(tail_in, 16)
            sp.dma_start(w3[:, :], w3_in).then_inc(tail_in, 16)
            sp.dma_start(dense[:, :], dense_in).then_inc(tail_in, 16)

            def next_indices(T):
                sp.wait_ge(rows_used, T)
                sp.dma_start(idx[:, :], ids[bass.ds(T * TILE_B, TILE_B), :]).then_inc(idx_in, 16)

            def scalars_of(T, g):
                S = T * GROUPS + g
                if g == 0:
                    sp.wait_ge(eT_ready, 2 * (T + 1))
                if not (isinstance(T, int) and S < 2):
                    sp.wait_ge(stt_done, STTS * CHUNKS * (S - 1) + CREDIT_STT)
                    sp.wait_ge(act_done, NACT * CHUNKS * (S - 1) + CREDIT_ACT)
                    sp.wait_ge(g_ps, CHUNKS * (S - 1) + CREDIT_ONE)
                src = eT[:, g * CHUNKS:(g + 1) * CHUNKS, :]
                sp.dma_start(eTg[:, g % 2, :, :], src).then_inc(eTg_in[g % 2], 16)
                for b in range(CHUNK_B):
                    n = slice(b * D, (b + 1) * D)
                    sp.dma_start(eBlk[n, g % 2, :, b, 0:M],
                                 eT[n, g * CHUNKS:(g + 1) * CHUNKS, :]).then_inc(eBlk_in[g % 2], 16)

            next_indices(1)
            sp.wait_ge(blk_clear, 3)
            for g in range(GROUPS):
                scalars_of(0, g)
            next_indices(2)
            with sp.Fori(1, TILES - 2) as T:
                for g in range(GROUPS):
                    scalars_of(T, g)
                next_indices(T + 2)
            with sp.Fori(TILES - 2, TILES) as T:
                for g in range(GROUPS):
                    scalars_of(T, g)
            sp.wait_ge(mlp_act, 14)
            sp.dma_start(out.rearrange("b one -> one b"), y[:, :]).then_inc(stored, 16)
            sp.wait_ge(stored, 16)

        @block.gpsimd
        def _(pool):
            pool.sem_inc(add_done, CREDIT_ADD)

            def gather(f):
                pool.indirect_dma_start(rows[:, f, :], None, tables[f],
                                        bass.IndirectOffsetOnAxis(idx[:, f:f + 1], 0)
                                        ).then_inc(gathered, 16)

            pool.wait_ge(idx_in, 16)
            for f in range(TABLES):
                gather(f)
            pool.memset(eBlk[:, :, :, :, :], 0.0).then_inc(blk_clear, 1)
            pool.wait_ge(blk_clear, 1)
            pool.wait_ge(consts_in, 48)
            for slot in range(2):
                pool.tensor_copy(eBlk[:, slot, :, :, M],
                                 mask[:, None, :].to_broadcast([128, CHUNKS, CHUNK_B])
                                 ).then_inc(blk_clear, 1)

            early, late = TILE_CHUNKS - CHUNKS, 10
            ahead = [3] * CHUNKS
            behind = [3] * 8 + [2] * 2
            assert sum(ahead) + sum(behind) == TABLES
            fields = {}
            f = 0
            for ch, n in [*zip(range(early, TILE_CHUNKS), ahead), *zip(range(late), behind)]:
                fields[ch] = list(range(f, f + n))
                f += n

            def tile(T, gather_next, gather_after):
                for ch in range(TILE_CHUNKS):
                    C = T * TILE_CHUNKS + ch
                    acc = part[:, ch % 2, 0:BANK_M, :].rearrange("p a h -> p (a h)")
                    due = list(fields.get(ch, ())) if (gather_after if ch >= early
                                                       else gather_next) else []
                    if ch == early and due:
                        pool.wait_ge(idx_in, 16 * (T + 3))
                    for i in range(1, NACT):
                        k = ch * NACT + i
                        pool.wait_ge(act_done, NACT * C + i + 1 + CREDIT_ACT)
                        if i == 1:
                            pool.wait_ge(x2_ready, C)
                            a, b_ = scaled[:, (k - 1) % 4, :], scaled[:, k % 4, :]
                        else:
                            pool.wait_ge(add_done, ADDS * C + (i - 1) + CREDIT_ADD)
                            a, b_ = acc, scaled[:, k % 4, :]
                        pool.tensor_tensor(acc, a, b_, ALU.add).then_inc(add_done, 1)
                        if due and i in (1, 3, 5):
                            gather(due.pop(0))

            pool.wait_ge(idx_in, 32)
            for ch in range(early, TILE_CHUNKS):
                for f in fields[ch]:
                    gather(f)
            tile(0, True, True)
            with pool.Fori(1, TILES - 2) as T:
                tile(T, True, True)
            tile(TILES - 2, True, False)
            tile(TILES - 1, False, False)

        @block.vector
        def _(dve):
            dve.sem_inc(stt_done, CREDIT_STT)
            dve.sem_inc(x2_ready, CREDIT_ONE)
            dve.memset(eHL[:, :, :].bitcast(f32), 0.0).then_inc(sel_ready, 1)
            dve.wait_ge(consts_in, 48)
            dve.tensor_copy(sel[:, :], sel_raw[:, :]).then_inc(sel_ready, 1)
            dve.wait_ge(w0_in, 32)
            dve.tensor_tensor(w0a, w0a, w0b, ALU.add).then_inc(w0_sum, 1)
            dve.wait_ge(w0_high, 1)
            dve.tensor_tensor(w0L[:, :, :].rearrange("p j h -> p (j h)"), w0a,
                              w0H[:, :, :].rearrange("p j h -> p (j h)").bitcast(f32),
                              ALU.subtract).then_inc(k_ready, 1)
            dve.wait_ge(w0_high, 2)
            dve.tensor_tensor(k1L[:, :], k1raw, k1H[:, :].bitcast(f32),
                              ALU.subtract).then_inc(k_ready, 1)

            def prep_l(T, r):
                dve.wait_ge(prep_high, 4 * T + r + 1)
                src = pSel[r % 2][0:M, :].rearrange("m (d b) -> m b d", d=4)
                dve.tensor_tensor(eHL[LO:EK, :, 4 * r:4 * r + 4], src,
                                  eHL[0:M, :, 4 * r:4 * r + 4].bitcast(f32),
                                  ALU.subtract).then_inc(prep_low, 1)

            def product(S, j):
                dve.wait_ge(shift_ps, BLOCKS * S + j + 1)
                if j == 0:
                    dve.wait_ge(rep_ready, S + 1)
                used = BLOCKS * S + max(j - 1, 0)
                dve.wait_ge(prodH_ready, used)
                dve.wait_ge(prodL_ready, used)
                dve.tensor_tensor(prod[:, j % 2, :], pSel[(j + 1) % 2][0:PR, :], eRep[:, :],
                                  ALU.mult).then_inc(prod_ready, 1)

            def product_l(S, j):
                dve.wait_ge(prodH_ready, BLOCKS * S + j + 1)
                dve.wait_ge(prod_used, BLOCKS * S + max(j - 1, 0))
                dve.tensor_tensor(prodL[:, j % 2, :], prod[:, j % 2, :],
                                  prodH[:, j % 2, :].bitcast(f32),
                                  ALU.subtract).then_inc(prodL_ready, 1)

            def x_low(S, part_):
                lo, hi = ((0, 3 * NC), (3 * NC, NG))[part_]
                dve.wait_ge(xH_ready, 2 * S + part_ + 1)
                if part_:
                    dve.tensor_reduce(z1[:, bass.ds(S * GROUP_B, GROUP_B)],
                                      pX1[:, :].rearrange("h (b d) -> h b d", d=D),
                                      AX.X, ALU.add)
                dve.tensor_tensor(xL[:, lo:hi], pX1[:, lo:hi], xH[:, lo:hi].bitcast(f32),
                                  ALU.subtract).then_inc(xL_ready, 1)

            def sum_x2(C, slot):
                dve.wait_ge(add_done, ADDS * (C + 1) + CREDIT_ADD)
                dve.wait_ge(stt_done, STTS * (C + 1) + CREDIT_STT)
                dve.wait_ge(g_ps, C)
                dve.tensor_reduce(x2[:, slot, :], part[:, slot, :, :].rearrange("p a h -> p h a"),
                                  AX.X, ALU.add).then_inc(x2_ready, 1)

            def sum_z3(T):
                dve.wait_ge(z3_copied, 3 * (T + 1))
                dve.tensor_reduce(z3[:, bass.ds(T * TILE_B, TILE_B)],
                                  z3p[:, :, :].rearrange("h a b -> h b a"), AX.X,
                                  ALU.add).then_inc(z3_ready, 1)

            def group(T, g, nxt, prep, first, zero):
                S = T * GROUPS + g

                def bank_work(s):
                    c, i = divmod(s, STEPS)
                    if i not in DVE_STEPS:
                        return
                    C = S * CHUNKS + c
                    k = DVE_STEPS.index(i)
                    if s == 0:
                        dve.wait_ge(eTg_in[g % 2], 16 * group_count(T, g))
                    if k == 0:
                        dve.wait_ge(x2_ready, C)
                    dve.wait_ge(y_dve, NDVE * C + k + 1)
                    for q in range(BANK_M):
                        u = k * BANK_M + q
                        scalar = eTg[:, g % 2, c, i * BANK_M + q:i * BANK_M + q + 1]
                        y_q = Y[s % 4][:, q * H:(q + 1) * H]
                        acc = part[:, c % 2, BANK_M + u % 2, :]
                        if u < 2:
                            dve.tensor_scalar(acc, y_q, scalar, None,
                                              ALU.mult).then_inc(stt_done, 1)
                        else:
                            dve.wait_ge(stt_done, STTS * C + u - 1 + CREDIT_STT)
                            dve.scalar_tensor_tensor(acc, y_q, scalar, acc, ALU.mult,
                                                     ALU.add).then_inc(stt_done, 1)

                others = [(3, lambda: x_low(S, 1))]
                for c in range(CHUNKS):
                    if not (first and c == 0):
                        others.append((c * STEPS + 6, lambda c=c: sum_x2(
                            S * CHUNKS + c - 1, (c + 1) % 2)))
                if prep:
                    for r in range(4):
                        others.append((PREP_AT[r] + 3, lambda r=r: prep_l(T + 1, r)))
                if g == 1 and not zero:
                    others.append((10, lambda: sum_z3(T - 1)))
                if nxt:
                    for j, at in enumerate(SHIFT_AT):
                        others.append((at + PRODUCT, lambda j=j: product(S + 1, j)))
                        others.append((at + LOW, lambda j=j: product_l(S + 1, j)))
                    others.append((35, lambda: x_low(S + 1, 0)))
                in_steps(bank_work, others)

            def tile(T, first, last):
                for g in range(GROUPS):
                    end = g == GROUPS - 1
                    group(T, g, not (last and end), g == 2 and not last, first and g == 0, first)

            for r in range(4):
                prep_l(0, r)
            for j in range(BLOCKS + 1):
                if j < BLOCKS:
                    product(0, j)
                if j:
                    product_l(0, j - 1)
            x_low(0, 0)
            all_tiles(dve, tile)
            sum_x2(TILES * TILE_CHUNKS - 1, 1)
            sum_z3(TILES - 1)

        @block.scalar
        def _(act):
            act.sem_inc(act_done, CREDIT_ACT)
            act.preload_act_table(ACT.Relu)
            act.wait_ge(w0_sum, 1)
            act.activation(w0H[:, :, :].rearrange("p j h -> p (j h)"), w0a,
                           ACT.Copy).then_inc(w0_high, 1)
            act.wait_ge(k1_loaded, 16)
            act.activation(k1H[:, :], k1raw, ACT.Copy).then_inc(w0_high, 1)

            def prep_h(T, r):
                act.wait_ge(prep_ps, 6 * T + r + 1)
                if isinstance(T, int) and T == 0:
                    act.wait_ge(sel_ready, 1)
                src = pSel[r % 2][0:M, :].rearrange("m (d b) -> m b d", d=4)
                act.activation(eHL[0:M, :, 4 * r:4 * r + 4], src, ACT.Copy).then_inc(prep_high, 1)

            def prep_eT(T, r):
                act.wait_ge(prep_ps, 6 * T + 4 + r + 1)
                if r == 0 and not (isinstance(T, int) and T == 0):
                    act.wait_ge(eTg_in[1], 16 * (GROUPS // 2) * T)
                    act.wait_ge(eBlk_in[0], 16 * CHUNK_B * (GROUPS // 2) * T)
                    act.wait_ge(eBlk_in[1], 16 * CHUNK_B * (GROUPS // 2) * T)
                half = TILE_CHUNKS // 2
                act.activation(eT[:, r * half:(r + 1) * half, :].rearrange("n c m -> n (c m)"),
                               pSel[r][:, 0:half * M], ACT.Copy).then_inc(eT_ready, 1)

            def rep(S):
                act.wait_ge(rep_ps, S + 1)
                act.activation(eRep[:, :], pSel[0][0:PR, :], ACT.Copy).then_inc(rep_ready, 1)

            def product_h(S, j):
                act.wait_ge(prod_ready, BLOCKS * S + j + 1)
                act.wait_ge(prod_used, BLOCKS * S + max(j - 1, 0))
                act.activation(prodH[:, j % 2, :], prod[:, j % 2, :],
                               ACT.Copy).then_inc(prodH_ready, 1)

            def x_high(S, part_):
                lo, hi = ((0, 3 * NC), (3 * NC, NG))[part_]
                act.wait_ge(prod_used, BLOCKS * (S + 1))
                act.activation(xH[:, lo:hi], pX1[:, lo:hi], ACT.Copy).then_inc(xH_ready, 1)

            def copy_G(C, T, ch):
                act.wait_ge(g_ps, C + 1 + CREDIT_ONE)
                dst = G[:, bass.ds(T % 2, 1), :, ch * CHUNK_B:(ch + 1) * CHUNK_B]
                act.activation(dst.rearrange("h one m b -> h (one b) m"),
                               pG[:, 0:CHUNK_B * GM].rearrange("h (b m) -> h b m", m=GM),
                               ACT.Copy).then_inc(g_copied, 1)

            def copy_z2(T):
                act.wait_ge(g_copied, TILE_CHUNKS * (T + 1))
                act.activation(z2[:, bass.ds(T * TILE_B, TILE_B)],
                               G[:, bass.ds(T % 2, 1), M, :].rearrange("h one b -> h (one b)"),
                               ACT.Copy).then_inc(z2_ready, 1)

            def copy_z3(T, w):
                act.wait_ge(z3_ps, 3 * T + w + 1)
                if w == 0 and not (isinstance(T, int) and T == 0):
                    act.wait_ge(z3_ready, T)
                act.activation(z3p[:, w, :], pG[:, 0:TILE_B], ACT.Copy).then_inc(z3_copied, 1)

            def group(T, g, nxt, prep, first, zero):
                S = T * GROUPS + g

                def bank_work(s):
                    c, i = divmod(s, STEPS)
                    if i not in ACT_STEPS:
                        return
                    C = S * CHUNKS + c
                    k = ACT_STEPS.index(i)
                    if s == ACT_STEPS[0]:
                        act.wait_ge(eTg_in[g % 2], 16 * group_count(T, g))
                    act.wait_ge(add_done, ADDS * C + min(k, 4))
                    act.wait_ge(y_act, NACT * C + k + 1)
                    for q in range(BANK_M):
                        a = act.activation(scaled[:, (c * NACT + k) % 4, q * H:(q + 1) * H],
                                           Y[s % RING][:, q * H:(q + 1) * H], ACT.Copy,
                                           scale=eTg[:, g % 2, c, i * BANK_M + q:i * BANK_M + q + 1])
                    a.then_inc(act_done, 1)

                others = [(2, lambda: x_high(S, 1))]
                for c in range(CHUNKS):
                    ch = g * CHUNKS + c - 2
                    if not (first and c < 2):
                        others.append((c * STEPS + 2, lambda c=c, ch=ch: copy_G(
                            S * CHUNKS + c - 2, T if ch >= 0 else T - 1, ch % TILE_CHUNKS)))
                if g == 0 and not zero:
                    others.append((14, lambda: copy_z2(T - 1)))
                for w, (zg, at) in enumerate(Z3_AT):
                    if g == zg and not zero:
                        others.append((at + 6, lambda w=w: copy_z3(T - 1, w)))
                if prep:
                    for r in range(4):
                        others.append((PREP_AT[r] + 2, lambda r=r: prep_h(T + 1, r)))
                    for r in range(2):
                        others.append((PREP_AT[4 + r] + 1, lambda r=r: prep_eT(T + 1, r)))
                if nxt:
                    others.append((1, lambda: rep(S + 1)))
                    for j, at in enumerate(SHIFT_AT):
                        others.append((at + HIGH, lambda j=j: product_h(S + 1, j)))
                    others.append((34, lambda: x_high(S + 1, 0)))
                in_steps(bank_work, others)

            def tile(T, first, last):
                for g in range(GROUPS):
                    end = g == GROUPS - 1
                    group(T, g, not (last and end), g == 2 and not last, first and g == 0, first)

            for r in range(4):
                prep_h(0, r)
            prep_eT(0, 0)
            prep_eT(0, 1)
            rep(0)
            for j in range(BLOCKS):
                product_h(0, j)
            x_high(0, 0)
            all_tiles(act, tile)
            for ch in range(TILE_CHUNKS - 2, TILE_CHUNKS):
                copy_G((TILES - 1) * TILE_CHUNKS + ch, TILES - 1, ch)
            copy_z2(TILES - 1)
            for w in range(3):
                copy_z3(TILES - 1, w)

            act.wait_ge(tail_in, 128)
            n = 0
            banks = [Y[0], Y[1], Y[2], Y[3]]
            for half in range(2):
                for o in range(4):
                    n += 1
                    act.wait_ge(mlp_ps, n)
                    act.activation(h1[:, o, :], banks[(n - 1) % 4][:, :], ACT.Relu,
                                   bias=b1[:, o:o + 1]).then_inc(mlp_act, 1)
                for o in range(2):
                    n += 1
                    act.wait_ge(mlp_ps, n)
                    act.activation(h2[:, o, :], banks[(n - 1) % 4][:, :], ACT.Relu,
                                   bias=b2[:, o:o + 1]).then_inc(mlp_act, 1)
                n += 1
                act.wait_ge(mlp_ps, n)
                act.activation(y[:, half * 512:(half + 1) * 512], banks[(n - 1) % 4][0:1, :],
                               ACT.Copy).then_inc(mlp_act, 1)

        @block.tensor
        def _(pe):
            pe.sem_inc(g_ps, CREDIT_ONE)

            def prep(T, r):
                ps = pSel[r % 2]
                if r < 2:
                    if r == 0:
                        pe.wait_ge(gathered, 16 * TABLES * (T + 1))
                    pe.wait_ge(prod_ready, BLOCKS * GROUPS * T)
                else:
                    pe.wait_ge(prep_low, 4 * T + min(r - 1, 4) + (r == 4))
                if r < 4:
                    for q in range(4):
                        a = pe.matmul(ps[0:M, q * TILE_B:(q + 1) * TILE_B], rows[:, :, 4 * r + q],
                                      ident[:, :], start=True, stop=True)
                    a.then_inc(prep_ps, 1)
                    if r == 3:
                        pe.wait_ge(prep_ps, 6 * T + 4)
                        pe.sem_inc(rows_used, 1)
                else:
                    for q in range(TILE_CHUNKS // 2):
                        c = (r - 4) * (TILE_CHUNKS // 2) + q
                        a = pe.matmul(ps[:, q * M:(q + 1) * M],
                                      eHL[:, c * CHUNK_B:(c + 1) * CHUNK_B, :].rearrange(
                                          "k b d -> k (b d)"),
                                      sel[:, 8 * PR:8 * PR + M], start=True, stop=True)
                    a.then_inc(prep_ps, 1)

            def e_group(g):
                return eHL[:, g * GROUP_B:(g + 1) * GROUP_B, :].rearrange("k b d -> k (b d)")

            def replicate(S, g, prepT):
                if prepT is not None:
                    pe.wait_ge(eT_ready, 2 * prepT + 1)
                else:
                    pe.wait_ge(prod_ready, BLOCKS * S - 1)
                pe.matmul(pSel[0][0:PR, :], sel_m(0), e_group(g), start=True,
                          stop=True).then_inc(rep_ps, 1)

            def shift(S, g, j, prepT):
                if j == 0 and prepT is not None:
                    pe.wait_ge(eT_ready, 2 * prepT + 2)
                elif j == 0:
                    pe.wait_ge(prod_ready, BLOCKS * S)
                elif j == 1:
                    pe.wait_ge(rep_ready, S + 1)
                else:
                    pe.wait_ge(prod_ready, BLOCKS * S + j - 1)
                pe.matmul(pSel[(j + 1) % 2][0:PR, :], sel_m(1 + j), e_group(g), start=True,
                          stop=True).then_inc(shift_ps, 1)

            def add_block(S, j):
                pe.wait_ge(prodL_ready, BLOCKS * S + j + 1)
                if j == 0:
                    pe.wait_ge(xL_ready, 2 * S)
                pe.matmul(pX1[:, :], w0H[:, j, :], prodH[:, j % 2, :], start=j == 0, stop=False)
                pe.matmul(pX1[:, :], w0L[:, j, :], prodH[:, j % 2, :], start=False, stop=False)
                pe.matmul(pX1[:, :], w0H[:, j, :], prodL[:, j % 2, :], start=False,
                          stop=j == BLOCKS - 1).then_inc(prod_used, 1)

            def make_G(C, T, ch):
                g, c = divmod(ch, CHUNKS)
                slot = ch % 2
                pe.wait_ge(x2_ready, C + 1 + CREDIT_ONE)
                if c == 0:
                    pe.wait_ge(eBlk_in[g % 2], 16 * CHUNK_B * group_count(T, g))
                pe.wait_ge(g_copied, C)
                for w, (zg, at) in enumerate(Z3_AT):
                    if (g * GSTEPS + (c + 2) * STEPS + 1 - 11 < zg * GSTEPS + at
                            <= g * GSTEPS + (c + 2) * STEPS + 1):
                        if not (isinstance(T, int) and T == 0):
                            pe.wait_ge(z3_copied, 3 * (T - 1) + w + 1)
                pe.matmul(pG[:, 0:CHUNK_B * GM], x2[:, slot, :],
                          eBlk[:, g % 2, c, :, :].rearrange("n b m -> n (b m)"), start=True,
                          stop=True).then_inc(g_ps, 1)

            def z3_part(T, w, m0, m1, more=0):
                if m0 == Z3_M[w]:
                    pe.wait_ge(g_copied, TILE_CHUNKS * (T + 1) + more)
                for m in range(m0, m1):
                    a = pe.matmul(pG[:, 0:TILE_B], k2[:, m, :],
                                  G[:, bass.ds(T % 2, 1), m, :].rearrange("h one b -> h (one b)"),
                                  start=m == Z3_M[w], stop=m == Z3_M[w + 1] - 1)
                if m1 == Z3_M[w + 1]:
                    a.then_inc(z3_ps, 1)

            def group(T, g, nxt, prep_next, first, zero):
                S = T * GROUPS + g

                def bank_work(s):
                    c, i = divmod(s, STEPS)
                    if s == 0:
                        pe.wait_ge(xL_ready, 2 * S + 1)
                    if s == 3 * STEPS:
                        pe.wait_ge(xL_ready, 2 * S + 2)
                    if not (first and s < RING):
                        wait_bank_free(pe, S, s)
                    x, w = slice(c * NC, (c + 1) * NC), slice(i * 512, (i + 1) * 512)
                    pe.matmul(Y[s % RING][:, :], xH[:, x], k1H[:, w], start=True, stop=False)
                    pe.matmul(Y[s % RING][:, :], xH[:, x], k1L[:, w], start=False, stop=False)
                    pe.matmul(Y[s % RING][:, :], xL[:, x], k1H[:, w], start=False,
                              stop=True).then_inc(y_dve if i in DVE_STEPS else y_act, 1)

                others = []
                for c in range(CHUNKS):
                    ch = g * CHUNKS + c - 2
                    if not (first and c < 2):
                        others.append((c * STEPS + 1, lambda c=c, ch=ch: make_G(
                            S * CHUNKS + c - 2, T if ch >= 0 else T - 1, ch % TILE_CHUNKS)))
                for w, (zg, at) in enumerate(Z3_AT):
                    if g == zg and not zero:
                        ms = np.linspace(Z3_M[w], Z3_M[w + 1], 6).astype(int).tolist()
                        for q in range(5):
                            others.append((at + q, lambda w=w, a=ms[q], b=ms[q + 1]: z3_part(
                                T - 1, w, a, b, w + 1)))
                if prep_next:
                    for r, at in enumerate(PREP_AT):
                        others.append((at, lambda r=r: prep(T + 1, r)))
                if nxt:
                    gn = (g + 1) % GROUPS
                    prepared = T + 1 if gn == 0 else None
                    others.append((0, lambda: replicate(S + 1, gn, prepared)))
                    for j, at in enumerate(SHIFT_AT):
                        others.append((at, lambda j=j: shift(S + 1, gn, j, prepared)))
                        others.append((at + ADD, lambda j=j: add_block(S + 1, j)))
                in_steps(bank_work, others)

            def tile(T, first, last):
                for g in range(GROUPS):
                    end = g == GROUPS - 1
                    group(T, g, not (last and end), g == 2 and not last, first and g == 0, first)

            pe.wait_ge(consts_in, 48)
            for r in range(6):
                if r == 4:
                    pe.wait_ge(sel_ready, 2)
                prep(0, r)
            replicate(0, 0, 0)
            for j in range(BLOCKS + 1):
                if j < BLOCKS:
                    shift(0, 0, j, 0)
                if j == 1:
                    pe.wait_ge(k_ready, 1)
                if j:
                    add_block(0, j - 1)
            pe.wait_ge(k_ready, 2)
            all_tiles(pe, tile)
            for ch in range(TILE_CHUNKS - 2, TILE_CHUNKS):
                make_G((TILES - 1) * TILE_CHUNKS + ch, TILES - 1, ch)
            for w in range(3):
                if w:
                    pe.wait_ge(z3_copied, 3 * (TILES - 1) + w)
                z3_part(TILES - 1, w, Z3_M[w], Z3_M[w + 1])

            pe.wait_ge(tail_in, 128)
            pe.wait_ge(z3_ready, TILES)
            pe.wait_ge(z2_ready, TILES)
            pe.wait_ge(stt_done, STTS * TILES * TILE_CHUNKS + CREDIT_STT)
            pe.wait_ge(act_done, NACT * TILES * TILE_CHUNKS + CREDIT_ACT)
            n = 0
            for half in range(2):
                b = slice(half * 512, (half + 1) * 512)
                done = 7 * half
                for o in range(4):
                    oc = slice(o * 128, (o + 1) * 128)
                    ps = Y[n % 4]
                    if n >= 4:
                        pe.wait_ge(mlp_act, n - 3)
                    pe.matmul(ps[:, :], w1[:, 0, oc], z1[:, b], start=True, stop=False)
                    pe.matmul(ps[:, :], w1[:, 1, oc], z2[:, b], start=False, stop=False)
                    pe.matmul(ps[:, :], w1[:, 2, oc], z3[:, b], start=False, stop=False)
                    pe.matmul(ps[:, :], w1d[:, oc], dense[:, b], start=False,
                              stop=True).then_inc(mlp_ps, 1)
                    n += 1
                for o in range(2):
                    pe.wait_ge(mlp_act, done + 4)
                    for k in range(4):
                        a = pe.matmul(Y[n % 4][:, :], w2[:, k, o * 128:(o + 1) * 128],
                                      h1[:, k, :], start=k == 0, stop=k == 3)
                    a.then_inc(mlp_ps, 1)
                    n += 1
                pe.wait_ge(mlp_act, done + 6)
                for k in range(2):
                    a = pe.matmul(Y[n % 4][0:1, :], w3[:, k:k + 1], h2[:, k, :],
                                  start=k == 0, stop=k == 1)
                a.then_inc(mlp_ps, 1)
                n += 1


def _constants():
    sel = np.zeros((EK, 8 * PR + M), np.float32)
    for q in range(8):
        for r in range(REP):
            shift = 0 if q == 0 else REP * (q - 1) + r
            for a in range(M):
                for base in (0, LO):
                    sel[base + (a + shift) % M, q * PR + r * M + a] = 1.0
    for m in range(M):
        sel[m, 8 * PR + m] = sel[LO + m, 8 * PR + m] = 1.0
    mask = (np.arange(128)[:, None] // D == np.arange(CHUNK_B)[None, :]).astype(np.float32)
    return np.eye(128, dtype=np.float32), sel, mask


def kernel(**inputs):
    import concourse.bacc as bacc
    from concourse.bass_utils import run_bass_kernel_spmd

    x = {k: np.asarray(v) for k, v in inputs.items()}
    ident, sel, mask = _constants()
    k0 = x["L0_rec_k0"]
    a = np.arange(M)
    k0a = np.zeros((BLOCKS, REP, M, H), np.float32)
    k0b = np.zeros((BLOCKS, REP, M, H), np.float32)
    for s in range(BLOCKS * REP):
        k0a[s // REP, s % REP] = k0[:, a, (a + s) % M].T
        if 0 < s < M // 2:
            k0b[s // REP, s % REP] = k0[:, (a + s) % M, a].T

    def by_row(k):
        return np.ascontiguousarray(k.transpose(1, 2, 0, 3).reshape(PR, BLOCKS * H))

    arrays = {
        "ids": x["ids"],
        **{f"tbl_{f}": x[f"tbl_{f}"] for f in range(TABLES)},
        "ident": ident, "sel": sel, "mask": mask,
        "k0a": by_row(k0a), "k0b": by_row(k0b),
        "k1": x["L0_rec_k1"].transpose(1, 2, 0).reshape(H, M * H),
        "k2": x["L0_rec_k2"].transpose(1, 2, 0),
        "w1": x["W_top1"][0:3 * H].reshape(3, H, 512).transpose(1, 0, 2),
        "w1d": x["W_top1"][3 * H:],
        "b1": x["b_top1"].reshape(4, 128).T,
        "w2": x["W_top2"].reshape(4, 128, 256).transpose(1, 0, 2),
        "b2": x["b_top2"].reshape(2, 128).T,
        "w3": x["W_top3"].reshape(2, 128).T,
        "dense": x["dense_ctx"].T,
    }
    arrays = {f"in_{k}": np.ascontiguousarray(v) for k, v in arrays.items()}
    nc = bacc.Bacc("TRN2", target_bir_lowering=False, num_devices=1)
    aps = {k: nc.dram_tensor(k, v.shape, mybir.dt.from_np(v.dtype), kind="ExternalInput").ap()
           for k, v in arrays.items()}
    out = nc.dram_tensor("out", (B, 1), mybir.dt.float32, kind="ExternalOutput").ap()
    names = ("ident", "sel", "mask", "k0a", "k0b", "k1", "k2", "w1", "w1d", "b1", "w2", "b2",
             "w3", "dense")
    build(nc, aps["in_ids"], [aps[f"in_tbl_{f}"] for f in range(TABLES)],
          *[aps[f"in_{k}"] for k in names], out)
    r = run_bass_kernel_spmd(nc, [arrays], core_ids=[0])
    return r.results[0]["out"]
```

```python
from contextlib import ExitStack

import numpy as np

import concourse.bass as bass
from concourse import mybir

B, M, D, H = 1024, 40, 16, 128
TILE_B, GROUP_B, CHUNK_B = 128, 32, 8
TILES = B // TILE_B
GROUPS = TILE_B // GROUP_B
CHUNKS = GROUP_B // CHUNK_B
TILE_CHUNKS = GROUPS * CHUNKS
NG = GROUP_B * D
NC = CHUNK_B * D
BANK_M = 512 // H
STEPS = M // BANK_M
GSTEPS = STEPS * CHUNKS
DVE_STEPS = (0, 3, 5, 8)
ACT_STEPS = (1, 2, 4, 6, 7, 9)
NDVE, NACT = len(DVE_STEPS), len(ACT_STEPS)
SUMMED = NACT - 1
STTS = NDVE * BANK_M
ADDS = SUMMED - 1
RING = 5
REP = 3
PR = REP * M
BLOCKS = (M // 2 + 1) // REP
CHOSEN = 2
SLOTS = 4
GM = M + 1
TABLES = M
PARTIALS = BANK_M + 2 + BANK_M

PIECE = 256
PIECES = ((0, 256), (256, 512), (512, 768), (768, 896), (896, 1024))
OUTPUTS = 7
BESIDE = OUTPUTS * (len(PIECES) - 1)

CREDIT_STT = 2 * BANK_M
CREDIT_ACT = 2
CREDIT_ADD = 3
CREDIT_ONE = 1


def build(nc, ids, tables, ident_in, mask_in, select_in, k0a_in, k0b_in, k1_in, k2_in, w1_in,
          w1d_in, b1_in, w2_in, b2_in, w3_in, dense_in, out):
    f32, f32r, i32 = mybir.dt.float32, mybir.dt.float32r, mybir.dt.int32
    ALU, ACT, AX = mybir.AluOpType, mybir.ActivationFunctionType, mybir.AxisListType
    ctx = ExitStack()
    with ctx:
        def sb(name, shape, dt=f32):
            return ctx.enter_context(nc.sbuf_tensor(name, shape, dt))

        def sem(name):
            return ctx.enter_context(nc.semaphore(name))

        idx = sb("idx", [TILE_B, M], i32)
        rows = sb("rows", [TILE_B, M, D])
        ident = sb("ident", [128, 128])
        mask = sb("mask", [128, CHUNK_B])
        w0H = sb("w0H", [PR, BLOCKS, H], f32r)
        w0L = sb("w0L", [PR, BLOCKS, H], f32r)
        k1H = sb("k1H", [H, M * H], f32r)
        k1L = sb("k1L", [H, M * H], f32r)
        k2 = sb("k2", [H, M, H])
        b1 = sb("b1", [128, 4])
        b2 = sb("b2", [128, 2])
        w1 = sb("w1", [128, 3, 512])
        w1d = sb("w1d", [128, 512])[96:96 + D, :]
        w2 = sb("w2", [128, 4, 256])
        w3 = sb("w3", [128, 2])
        packed = sb("packed", [128, TILE_B * D])
        e = packed[0:M, :].rearrange("m (b d) -> m b d", d=D)
        dense = packed[96:96 + D, 0:B]
        y = packed[96:97, B:2 * B]
        eT = sb("eT", [128, TILE_CHUNKS, M])
        eTg = sb("eTg", [128, 2, CHUNKS, M])
        eRep = sb("eRep", [PR, NG])
        prod = sb("prod", [PR, SLOTS, NG])
        prodH = sb("prodH", [PR, 2, NG], f32r)
        prodL = sb("prodL", [PR, 2, NG], f32r)
        xH = sb("xH", [H, NG], f32r)
        xL = sb("xL", [H, NG], f32r)
        scaled = sb("scaled", [128, 4, BANK_M * H])
        part = sb("part", [128, 2, PARTIALS, H])
        x2 = sb("x2", [128, 2, H])
        eBlk = sb("eBlk", [128, 2, CHUNKS, CHUNK_B, GM])
        G = sb("G", [H, 2, GM, TILE_B])
        z1 = sb("z1", [H, B])
        z2 = sb("z2", [H, B])
        z3 = sb("z3", [H, B])
        h1 = sb("h1", [128, 4, PIECE])
        h2 = sb("h2", [128, 2, PIECE])
        Gflat = G[:, :, :, :].rearrange("p a m b -> p (a m b)")
        k1raw = Gflat[:, 0:M * H]
        w0a = Gflat[0:PR, M * H:M * H + BLOCKS * H]
        w0b = Gflat[0:PR, M * H + BLOCKS * H:M * H + 2 * BLOCKS * H]
        after = M * H + 2 * BLOCKS * H
        select = Gflat[0:M, after:after + (1 + CHOSEN) * PR]

        def bank(name):
            return ctx.enter_context(nc.psum_tensor(name, [128, 512], f32))

        Y = [bank(f"Y{i}") for i in range(RING)]
        pP = bank("pP")
        pX1, pG = bank("pX1"), bank("pG")

        FIRST_PREP = (Y[0], Y[1], Y[2], Y[3], Y[4], pP)
        FIRST_SEL = (Y[0], Y[1], Y[2])

        e2 = nc.dram_tensor("e2", (2 * M, B * D), f32, kind="Internal").ap()

        idx_in, consts_in, w0_in, k1_loaded, tail_in = map(
            sem, ("idx_in", "consts_in", "w0_in", "k1_loaded", "tail_in"))
        gathered = sem("gathered")
        gathered_most = sem("gathered_most")
        w0_sum = sem("w0_sum")
        w0_high = sem("w0_high")
        k_ready = sem("k_ready")
        prep_ps = sem("prep_ps")
        e_copied = sem("e_copied")
        e_stored = sem("e_stored")
        eT_ready = sem("eT_ready")
        sel_ps = sem("sel_ps")
        rep_copied = sem("rep_copied")
        rep_in = sem("rep_in")
        shift_in = [sem("shift_in01"), sem("shift_in23")]
        prod_ready = sem("prod_ready")
        prodH_ready = sem("prodH_ready")
        prodL_ready = sem("prodL_ready")
        prod_used = sem("prod_used")
        xH_ready = sem("xH_ready")
        xL_ready = sem("xL_ready")
        y_dve = sem("y_dve")
        y_act = sem("y_act")
        stt_done = sem("stt_done")
        act_done = sem("act_done")
        add_done = sem("add_done")
        x2_ready = sem("x2_ready")
        eTg_in = [sem("eTg_in0"), sem("eTg_in1")]
        eBlk_in = [sem("eBlk_in0"), sem("eBlk_in1")]
        g_ps = sem("g_ps")
        g_copied = sem("g_copied")
        z3_ps = sem("z3_ps")
        z3_ready = sem("z3_ready")
        z2_ready = sem("z2_ready")
        blk_clear = sem("blk_clear")
        mlp_ps = sem("mlp_ps")
        mlp_act = sem("mlp_act")
        stored = sem("stored")

        block = ctx.enter_context(nc.Block())

        PRODUCT_AT = [4 + 7 * j // 2 for j in range(BLOCKS)]
        HIGH, LOW, ADD = 2, 4, 9
        PREP_AT = (5, 10, 15, 20, 26, 32)
        Z3_FROM, Z3_TO, Z3_COPY = 22, 43, 45
        SUM_X2 = 6
        MAKE_G, COPY_G = 2, 3

        DENSE_FIRST = 4
        DENSE_AT = ([5 * n for n in range(DENSE_FIRST)] + [48 + 11 * n // 2 for n in range(20)]
                    + [GROUPS * GSTEPS] * 4)

        def dense_bank(n):
            return pP if n < BESIDE else Y[n % RING]

        MOST = TABLES - 5

        def wait_bank_free(pe, S, s):
            c, i = divmod(s - RING, STEPS)
            C = S * CHUNKS + c
            if i in DVE_STEPS:
                pe.wait_ge(stt_done, BANK_M * (NDVE * C + DVE_STEPS.index(i) + 1) + CREDIT_STT)
            else:
                pe.wait_ge(act_done, NACT * C + ACT_STEPS.index(i) + 1 + CREDIT_ACT)

        def group_count(T, g):
            return T * (GROUPS // 2) + g // 2 + 1

        def in_steps(bank_work, others):
            for s in range(GSTEPS):
                for at, what in others:
                    if at == s:
                        what()
                bank_work(s)
            for at, what in others:
                if at >= GSTEPS:
                    what()

        def all_tiles(eng, tile):
            tile(0, True, False)
            with eng.Fori(1, TILES - 1) as t:
                tile(t, False, False)
            tile(TILES - 1, False, True)

        @block.sync
        def _(sp):
            sp.dma_start(idx[:, :], ids[0:TILE_B, :]).then_inc(idx_in, 16)
            sp.dma_start(ident[:, :], ident_in).then_inc(consts_in, 16)
            sp.dma_start(select, select_in).then_inc(consts_in, 16)
            sp.dma_start(mask[:, :], mask_in).then_inc(consts_in, 16)
            sp.dma_start(w0a, k0a_in).then_inc(w0_in, 16)
            sp.dma_start(w0b, k0b_in).then_inc(w0_in, 16)
            sp.dma_start(k1raw, k1_in).then_inc(k1_loaded, 16)
            sp.dma_start(k2[:, :, :], k2_in).then_inc(tail_in, 16)
            sp.dma_start(b1[:, :], b1_in).then_inc(tail_in, 16)
            sp.dma_start(b2[:, :], b2_in).then_inc(tail_in, 16)
            sp.dma_start(w3[:, :], w3_in).then_inc(tail_in, 16)

            def store_e(T):
                sp.wait_ge(e_copied, 4 * (T + 1))
                dst = e2[:, bass.ds(T * TILE_B * D, TILE_B * D)]
                sp.dma_start(dst.rearrange("(two m) n -> m two n", two=2),
                             packed[0:M, None, :].to_broadcast([M, 2, TILE_B * D])
                             ).then_inc(e_stored, 16)

            def repeated(S, row, between):
                base = e2[row:row + 1, bass.ds(S * NG, NG)]
                return bass.AP(base.tensor, base.offset,
                               [(between * B * D, REP), (B * D, M), (1, NG)])

            def shifted(S, j0, n):
                for j in range(j0, j0 + n):
                    sp.dma_start(prod[:, j % SLOTS, :], repeated(S, REP * j, 1)
                                 ).then_inc(shift_in[j0 % SLOTS // 2], 16)

            def first_blocks(S):
                sp.wait_ge(prod_ready, BLOCKS * S)
                sp.dma_start(eRep[:, :], repeated(S, 0, 0)).then_inc(rep_in, 16)
                sp.wait_ge(prodL_ready, BLOCKS * S - 1)
                shifted(S, 0, 2)
                sp.wait_ge(prodL_ready, BLOCKS * S)
                shifted(S, 2, 2)

            def last_blocks(S):
                sp.wait_ge(prodL_ready, BLOCKS * S + 2)
                shifted(S, 4, 2)
                sp.wait_ge(prodL_ready, BLOCKS * S + 3)
                shifted(S, 6, 1)

            def next_indices(T):
                sp.wait_ge(prep_ps, 6 * (T - 1) + 4)
                sp.dma_start(idx[:, :], ids[bass.ds(T * TILE_B, TILE_B), :]).then_inc(idx_in, 16)

            def scalars_of(T, g):
                S = T * GROUPS + g
                if g == 0:
                    sp.wait_ge(eT_ready, 2 * (T + 1))
                if not (isinstance(T, int) and S < 2):
                    sp.wait_ge(stt_done, STTS * CHUNKS * (S - 1) + CREDIT_STT)
                    sp.wait_ge(act_done, NACT * CHUNKS * (S - 1) + CREDIT_ACT)
                    sp.wait_ge(g_ps, CHUNKS * (S - 1) + CREDIT_ONE)
                src = eT[:, g * CHUNKS:(g + 1) * CHUNKS, :]
                sp.dma_start(eTg[:, g % 2, :, :], src).then_inc(eTg_in[g % 2], 16)
                for b in range(CHUNK_B):
                    n = slice(b * D, (b + 1) * D)
                    sp.dma_start(eBlk[n, g % 2, :, b, 0:M],
                                 eT[n, g * CHUNKS:(g + 1) * CHUNKS, :]).then_inc(eBlk_in[g % 2], 16)

            def group(T, g, nxt, after, store, indices):
                S = T * GROUPS + g
                if nxt:
                    last_blocks(S + 1)
                    scalars_of(T + (g + 1) // GROUPS, (g + 1) % GROUPS)
                if store:
                    store_e(T + 1)
                    sp.wait_ge(e_stored, 16 * (T + 2))
                if indices:
                    next_indices(T + 2)
                if after:
                    first_blocks(S + 2)

            def tile(T, prepare, indices, last):
                for g in range(GROUPS):
                    group(T, g, not (last and g == GROUPS - 1), not (last and g >= GROUPS - 2),
                          g == 2 and prepare, g == 2 and indices)

            next_indices(1)
            store_e(0)
            sp.wait_ge(e_stored, 16)
            shifted(0, CHOSEN, SLOTS - CHOSEN)
            last_blocks(0)
            sp.wait_ge(blk_clear, 3)
            scalars_of(0, 0)
            first_blocks(1)
            sp.dma_start(w1[:, :, :], w1_in).then_inc(tail_in, 16)
            sp.dma_start(w1d, w1d_in).then_inc(tail_in, 16)
            sp.dma_start(w2[:, :, :], w2_in).then_inc(tail_in, 16)
            sp.dma_start(dense, dense_in).then_inc(tail_in, 16)
            tile(0, True, True, False)
            with sp.Fori(1, TILES - 2) as T:
                tile(T, True, True, False)
            tile(TILES - 2, True, False, False)
            tile(TILES - 1, False, False, True)

            sp.wait_ge(tail_in, 128)
            sp.wait_ge(mlp_act, OUTPUTS * len(PIECES))
            sp.dma_start(out.rearrange("b one -> one b"), y[:, :]).then_inc(stored, 16)
            sp.wait_ge(stored, 16)

        @block.gpsimd
        def _(pool):
            pool.sem_inc(add_done, CREDIT_ADD)

            def gather(f, done=gathered):
                pool.indirect_dma_start(rows[:, f, :], None, tables[f],
                                        bass.IndirectOffsetOnAxis(idx[:, f:f + 1], 0)
                                        ).then_inc(done, 16)

            pool.wait_ge(idx_in, 16)
            for f in range(TABLES):
                gather(f, gathered_most if f < MOST else gathered)
            pool.memset(eBlk[:, :, :, :, :], 0.0).then_inc(blk_clear, 1)
            pool.wait_ge(blk_clear, 1)
            pool.wait_ge(consts_in, 48)
            for slot in range(2):
                pool.tensor_copy(eBlk[:, slot, :, :, M],
                                 mask[:, None, :].to_broadcast([128, CHUNKS, CHUNK_B])
                                 ).then_inc(blk_clear, 1)

            early, late = 11, 8
            ahead = [3, 3, 3, 4, 4]
            behind = [3] * 7 + [2]
            assert sum(ahead) + sum(behind) == TABLES
            fields = {}
            f = 0
            for ch, n in [*zip(range(early, TILE_CHUNKS), ahead), *zip(range(late), behind)]:
                fields[ch] = list(range(f, f + n))
                f += n

            def tile(T, gather_next, gather_after):
                for ch in range(TILE_CHUNKS):
                    C = T * TILE_CHUNKS + ch
                    acc = part[:, ch % 2, 0:BANK_M, :].rearrange("p a h -> p (a h)")
                    due = list(fields.get(ch, ())) if (gather_after if ch >= early
                                                       else gather_next) else []
                    if ch == early and due:
                        pool.wait_ge(idx_in, 16 * (T + 3))
                    for i in range(1, SUMMED):
                        k = ch * SUMMED + i
                        pool.wait_ge(act_done, NACT * C + i + 1 + CREDIT_ACT)
                        if i == 1:
                            pool.wait_ge(x2_ready, C)
                            a, b_ = scaled[:, (k - 1) % 4, :], scaled[:, k % 4, :]
                        else:
                            pool.wait_ge(add_done, ADDS * C + (i - 1) + CREDIT_ADD)
                            a, b_ = acc, scaled[:, k % 4, :]
                        pool.tensor_tensor(acc, a, b_, ALU.add).then_inc(add_done, 1)
                        if due:
                            gather(due.pop(0))

            pool.wait_ge(idx_in, 32)
            for ch in range(early, TILE_CHUNKS):
                for f in fields[ch]:
                    gather(f)
            tile(0, True, True)
            with pool.Fori(1, TILES - 2) as T:
                tile(T, True, True)
            tile(TILES - 2, True, False)
            tile(TILES - 1, False, False)

        @block.vector
        def _(dve):
            dve.sem_inc(stt_done, CREDIT_STT)
            dve.sem_inc(x2_ready, CREDIT_ONE)
            dve.wait_ge(w0_in, 32)
            dve.tensor_tensor(w0a, w0a, w0b, ALU.add).then_inc(w0_sum, 1)
            dve.wait_ge(w0_high, 1)
            dve.tensor_tensor(w0L[:, :, :].rearrange("p j h -> p (j h)"), w0a,
                              w0H[:, :, :].rearrange("p j h -> p (j h)").bitcast(f32),
                              ALU.subtract).then_inc(k_ready, 1)
            dve.wait_ge(w0_high, 2)
            dve.tensor_tensor(k1L[:, :], k1raw, k1H[:, :].bitcast(f32),
                              ALU.subtract).then_inc(k_ready, 1)

            def product(S, j):
                if j == 0:
                    dve.wait_ge(rep_in, 16 * S)
                if j % 2 == 0:
                    per_group = 64 if j % SLOTS == 0 else 48
                    before = 16 * CHOSEN if j % SLOTS == 0 else 0
                    dve.wait_ge(shift_in[j % SLOTS // 2],
                                per_group * S + (32 if j < SLOTS else per_group) - before)
                p = prod[:, j % SLOTS, :]
                dve.tensor_tensor(p, p, eRep[:, :], ALU.mult).then_inc(prod_ready, 1)

            def first_product(j):
                if j == 0:
                    dve.wait_ge(rep_copied, 1)
                dve.wait_ge(sel_ps, j + 2)
                dve.tensor_tensor(prod[:, j % SLOTS, :], FIRST_SEL[1 + j][0:PR, :], eRep[:, :],
                                  ALU.mult).then_inc(prod_ready, 1)

            def product_l(S, j):
                dve.wait_ge(prodH_ready, BLOCKS * S + j + 1)
                dve.wait_ge(prod_used, BLOCKS * S + max(j - 1, 0))
                dve.tensor_tensor(prodL[:, j % 2, :], prod[:, j % SLOTS, :],
                                  prodH[:, j % 2, :].bitcast(f32),
                                  ALU.subtract).then_inc(prodL_ready, 1)

            def x_low(S, part_):
                lo, hi = ((0, 3 * NC), (3 * NC, NG))[part_]
                dve.wait_ge(xH_ready, 2 * S + part_ + 1)
                if part_:
                    dve.tensor_reduce(z1[:, bass.ds(S * GROUP_B, GROUP_B)],
                                      pX1[:, :].rearrange("h (b d) -> h b d", d=D),
                                      AX.X, ALU.add)
                dve.tensor_tensor(xL[:, lo:hi], pX1[:, lo:hi], xH[:, lo:hi].bitcast(f32),
                                  ALU.subtract).then_inc(xL_ready, 1)

            def sum_x2(C, slot):
                dve.wait_ge(add_done, ADDS * (C + 1) + CREDIT_ADD)
                dve.wait_ge(stt_done, STTS * (C + 1) + CREDIT_STT)
                dve.wait_ge(act_done, NACT * (C + 1) + CREDIT_ACT)
                dve.wait_ge(g_ps, C)
                dve.tensor_reduce(x2[:, slot, :], part[:, slot, :, :].rearrange("p a h -> p h a"),
                                  AX.X, ALU.add).then_inc(x2_ready, 1)

            def group(T, g, nxt, prep, first, zero):
                S = T * GROUPS + g

                def bank_work(s):
                    c, i = divmod(s, STEPS)
                    if i not in DVE_STEPS:
                        return
                    C = S * CHUNKS + c
                    k = DVE_STEPS.index(i)
                    if s == 0:
                        dve.wait_ge(eTg_in[g % 2], 16 * group_count(T, g))
                    if k == 0:
                        dve.wait_ge(x2_ready, C)
                    dve.wait_ge(y_dve, NDVE * C + k + 1)
                    for q in range(BANK_M):
                        u = k * BANK_M + q
                        scalar = eTg[:, g % 2, c, i * BANK_M + q:i * BANK_M + q + 1]
                        y_q = Y[s % RING][:, q * H:(q + 1) * H]
                        acc = part[:, c % 2, BANK_M + u % 2, :]
                        if u < 2:
                            dve.tensor_scalar(acc, y_q, scalar, None,
                                              ALU.mult).then_inc(stt_done, 1)
                        else:
                            dve.wait_ge(stt_done, STTS * C + u - 1 + CREDIT_STT)
                            dve.scalar_tensor_tensor(acc, y_q, scalar, acc, ALU.mult,
                                                     ALU.add).then_inc(stt_done, 1)

                others = [(3, lambda: x_low(S, 1))]
                if nxt:
                    for j, at in enumerate(PRODUCT_AT):
                        others.append((at, lambda j=j: product(S + 1, j)))
                        others.append((at + LOW, lambda j=j: product_l(S + 1, j)))
                    others.append((35, lambda: x_low(S + 1, 0)))
                for c in range(CHUNKS):
                    if not (first and c == 0):
                        others.append((c * STEPS + SUM_X2, lambda c=c: sum_x2(
                            S * CHUNKS + c - 1, (c + 1) % 2)))
                in_steps(bank_work, others)

            def tile(T, first, last):
                for g in range(GROUPS):
                    end = g == GROUPS - 1
                    group(T, g, not (last and end), g == 2 and not last, first and g == 0, first)

            for j in range(CHOSEN):
                first_product(j)
            for j in range(CHOSEN):
                product_l(0, j)
            for j in range(CHOSEN, BLOCKS + 1):
                if j < BLOCKS:
                    product(0, j)
                if j > CHOSEN:
                    product_l(0, j - 1)
            x_low(0, 0)
            all_tiles(dve, tile)
            sum_x2(TILES * TILE_CHUNKS - 1, 1)

        @block.scalar
        def _(act):
            act.sem_inc(act_done, CREDIT_ACT)
            act.preload_act_table(ACT.Relu)
            act.wait_ge(w0_sum, 1)
            act.activation(w0H[:, :, :].rearrange("p j h -> p (j h)"), w0a,
                           ACT.Copy).then_inc(w0_high, 1)
            act.wait_ge(k1_loaded, 16)
            act.activation(k1H[:, :], k1raw, ACT.Copy).then_inc(w0_high, 1)

            def prep_e(T, r, bank=pP):
                act.wait_ge(prep_ps, 6 * T + r + 1)
                if r == 0 and not (isinstance(T, int) and T == 0):
                    act.wait_ge(e_stored, 16 * T)
                src = bank[0:M, :].rearrange("m (d b) -> m b d", d=4)
                act.activation(e[:, :, 4 * r:4 * r + 4], src, ACT.Copy).then_inc(e_copied, 1)

            def prep_eT(T, r, bank=pP):
                act.wait_ge(prep_ps, 6 * T + 4 + r + 1)
                if r == 0 and not (isinstance(T, int) and T == 0):
                    act.wait_ge(eTg_in[1], 16 * (GROUPS // 2) * T)
                    act.wait_ge(eBlk_in[0], 16 * CHUNK_B * (GROUPS // 2) * T)
                    act.wait_ge(eBlk_in[1], 16 * CHUNK_B * (GROUPS // 2) * T)
                half = TILE_CHUNKS // 2
                act.activation(eT[:, r * half:(r + 1) * half, :].rearrange("n c m -> n (c m)"),
                               bank[:, 0:half * M], ACT.Copy).then_inc(eT_ready, 1)

            def product_h(S, j):
                act.wait_ge(prod_ready, BLOCKS * S + j + 1)
                act.wait_ge(prod_used, BLOCKS * S + max(j - 1, 0))
                act.activation(prodH[:, j % 2, :], prod[:, j % SLOTS, :],
                               ACT.Copy).then_inc(prodH_ready, 1)

            def x_high(S, part_):
                lo, hi = ((0, 3 * NC), (3 * NC, NG))[part_]
                if part_ == 0:
                    act.wait_ge(prod_used, BLOCKS * (S + 1))
                else:
                    act.wait_ge(xL_ready, 2 * S + 1)
                act.activation(xH[:, lo:hi], pX1[:, lo:hi], ACT.Copy).then_inc(xH_ready, 1)

            def copy_G(C, T, ch):
                act.wait_ge(g_ps, C + 1 + CREDIT_ONE)
                dst = G[:, bass.ds(T % 2, 1), :, ch * CHUNK_B:(ch + 1) * CHUNK_B]
                act.activation(dst.rearrange("h one m b -> h (one b) m"),
                               pG[:, 0:CHUNK_B * GM].rearrange("h (b m) -> h b m", m=GM),
                               ACT.Copy).then_inc(g_copied, 1)

            def copy_z2(T):
                act.wait_ge(g_copied, TILE_CHUNKS * (T + 1))
                act.activation(z2[:, bass.ds(T * TILE_B, TILE_B)],
                               G[:, bass.ds(T % 2, 1), M, :].rearrange("h one b -> h (one b)"),
                               ACT.Copy).then_inc(z2_ready, 1)

            def activate(n):
                piece, k = divmod(n, OUTPUTS)
                lo, hi = PIECES[piece]
                w = hi - lo
                ps = dense_bank(n)[:, 0:w]
                if n == 0:
                    act.wait_ge(tail_in, 128)
                act.wait_ge(mlp_ps, n + 1)
                if k < 4:
                    a = act.activation(h1[:, k, 0:w], ps, ACT.Relu, bias=b1[:, k:k + 1])
                elif k < 6:
                    a = act.activation(h2[:, k - 4, 0:w], ps, ACT.Relu, bias=b2[:, k - 4:k - 3])
                else:
                    a = act.activation(y[:, lo:hi], ps[0:1, :], ACT.Copy)
                a.then_inc(mlp_act, 1)

            def copy_z3(T, bank):
                act.wait_ge(z3_ps, T + 1)
                act.activation(z3[:, bass.ds(T * TILE_B, TILE_B)], bank[:, 0:TILE_B],
                               ACT.Copy).then_inc(z3_ready, 1)

            def group(T, g, nxt, prep, first, zero, last):
                S = T * GROUPS + g

                def bank_work(s):
                    c, i = divmod(s, STEPS)
                    if i not in ACT_STEPS:
                        return
                    C = S * CHUNKS + c
                    k = ACT_STEPS.index(i)
                    if s == ACT_STEPS[0]:
                        act.wait_ge(eTg_in[g % 2], 16 * group_count(T, g))
                    if k < SUMMED:
                        act.wait_ge(add_done, ADDS * C + k)
                        dst = scaled[:, (c * SUMMED + k) % 4, :]
                    else:
                        act.wait_ge(x2_ready, C)
                        dst = part[:, c % 2, BANK_M + 2:PARTIALS, :].rearrange("n a h -> n (a h)")
                    act.wait_ge(y_act, NACT * C + k + 1)
                    for q in range(BANK_M):
                        a = act.activation(dst[:, q * H:(q + 1) * H],
                                           Y[s % RING][:, q * H:(q + 1) * H], ACT.Copy,
                                           scale=eTg[:, g % 2, c, i * BANK_M + q:i * BANK_M + q + 1])
                    a.then_inc(act_done, 1)

                others = [(1, lambda: x_high(S, 1))]
                for c in range(CHUNKS):
                    ch = g * CHUNKS + c - 2
                    if not (first and c < 2):
                        others.append((c * STEPS + COPY_G, lambda c=c, ch=ch: copy_G(
                            S * CHUNKS + c - 2, T if ch >= 0 else T - 1, ch % TILE_CHUNKS)))
                if g == 0 and not zero:
                    others.append((STEPS + COPY_G + 1, lambda: copy_z2(T - 1)))
                if g == Z3_COPY // GSTEPS and not zero:
                    others.append((Z3_COPY % GSTEPS, lambda: copy_z3(T - 1, pP)))
                if prep:
                    for r in range(4):
                        others.append((PREP_AT[r] + 1, lambda r=r: prep_e(T + 1, r)))
                    for r in range(2):
                        others.append((PREP_AT[4 + r] + 1, lambda r=r: prep_eT(T + 1, r)))
                if last:
                    for n, at in enumerate(DENSE_AT):
                        if min(at // GSTEPS, GROUPS - 1) == g:
                            others.append((at - g * GSTEPS + 2, lambda n=n: activate(n)))
                if nxt:
                    for j, at in enumerate(PRODUCT_AT):
                        others.append((at + HIGH, lambda j=j: product_h(S + 1, j)))
                    others.append((34, lambda: x_high(S + 1, 0)))
                in_steps(bank_work, others)

            def tile(T, first, last):
                for g in range(GROUPS):
                    end = g == GROUPS - 1
                    group(T, g, not (last and end), g == 2 and not last, first and g == 0, first,
                          last)

            for r in range(4):
                prep_e(0, r, FIRST_PREP[r])
            act.wait_ge(sel_ps, 1)
            act.activation(eRep[:, :], FIRST_SEL[0][0:PR, :], ACT.Copy).then_inc(rep_copied, 1)
            for j in range(CHOSEN):
                product_h(0, j)
            for r in range(2):
                prep_eT(0, r, FIRST_PREP[4 + r])
            for j in range(CHOSEN, BLOCKS):
                product_h(0, j)
            x_high(0, 0)
            all_tiles(act, tile)
            for ch in range(TILE_CHUNKS - 2, TILE_CHUNKS):
                copy_G((TILES - 1) * TILE_CHUNKS + ch, TILES - 1, ch)
            copy_z2(TILES - 1)
            copy_z3(TILES - 1, pG)
            for n in range(BESIDE, OUTPUTS * len(PIECES)):
                activate(n)

        @block.tensor
        def _(pe):
            pe.sem_inc(g_ps, CREDIT_ONE)

            def prep(T, r, bank=pP):
                pe.wait_ge(consts_in, 48)
                if r == 0:
                    pe.wait_ge(gathered, 16 * (TABLES * (T + 1) - MOST))
                if bank is pP and not (isinstance(T, int) and T == 0):
                    if r == 0:
                        pe.wait_ge(eT_ready, 2 * T)
                        if not (isinstance(T, int) and T == 1):
                            pe.wait_ge(z3_ready, T - 1)
                    elif r < 4:
                        pe.wait_ge(e_copied, 4 * T + r)
                    elif r == 5:
                        pe.wait_ge(eT_ready, 2 * T + 1)
                if r == 4:
                    pe.wait_ge(e_copied, 4 * T + 4)
                if r < 4:
                    for q in range(4):
                        ps, x = bank[0:M, q * TILE_B:(q + 1) * TILE_B], rows[:, :, 4 * r + q]
                        if q == 0:
                            pe.matmul(ps, x, ident[:, :], start=True, stop=True)
                        else:
                            a = pe.transpose(ps, x, ident[:, :])
                else:
                    half = TILE_CHUNKS // 2
                    for q in range(half):
                        c = (r - 4) * half + q
                        ps = bank[:, q * M:(q + 1) * M]
                        x = e[:, c * CHUNK_B:(c + 1) * CHUNK_B, :].rearrange("m b d -> m (b d)")
                        if q == 0:
                            pe.matmul(ps, x, ident[0:M, 0:M], start=True, stop=True)
                        else:
                            a = pe.transpose(ps, x, ident[0:M, 0:M])
                a.then_inc(prep_ps, 1)

            def choose(i):
                pe.matmul(FIRST_SEL[i][0:PR, :], select[:, i * PR:(i + 1) * PR], packed[0:M, 0:NG],
                          start=True, stop=True).then_inc(sel_ps, 1)

            def add_block(S, j):
                pe.wait_ge(prodL_ready, BLOCKS * S + j + 1)
                if j == 0:
                    pe.wait_ge(xL_ready, 2 * S)
                pe.matmul(pX1[:, :], w0H[:, j, :], prodH[:, j % 2, :], start=j == 0, stop=False)
                pe.matmul(pX1[:, :], w0L[:, j, :], prodH[:, j % 2, :], start=False, stop=False)
                pe.matmul(pX1[:, :], w0H[:, j, :], prodL[:, j % 2, :], start=False,
                          stop=j == BLOCKS - 1).then_inc(prod_used, 1)

            def make_G(C, T, ch):
                g, c = divmod(ch, CHUNKS)
                slot = ch % 2
                pe.wait_ge(x2_ready, C + 1 + CREDIT_ONE)
                if c == 0:
                    pe.wait_ge(eBlk_in[g % 2], 16 * CHUNK_B * group_count(T, g))
                pe.wait_ge(g_copied, C)
                pe.matmul(pG[:, 0:CHUNK_B * GM], x2[:, slot, :],
                          eBlk[:, g % 2, c, :, :].rearrange("n b m -> n (b m)"), start=True,
                          stop=True).then_inc(g_ps, 1)

            def z3_part(T, m0, m1, bank):
                if m0 == 0:
                    pe.wait_ge(g_copied, TILE_CHUNKS * (T + 1))
                    if bank is pP:
                        pe.wait_ge(eT_ready, 2 * (T + 2))
                        if isinstance(T, int) and T == TILES - 2:
                            pe.wait_ge(mlp_act, DENSE_FIRST)
                for m in range(m0, m1):
                    a = pe.matmul(bank[:, 0:TILE_B], k2[:, m, :],
                                  G[:, bass.ds(T % 2, 1), m, :].rearrange("h one b -> h (one b)"),
                                  start=m == 0, stop=m == M - 1)
                if m1 == M:
                    a.then_inc(z3_ps, 1)

            def dense_begin(n):
                k = n - BESIDE
                if k == 0:
                    pe.wait_ge(xL_ready, 2 * TILES * GROUPS)
                    pe.wait_ge(stt_done, STTS * TILES * TILE_CHUNKS + CREDIT_STT)
                    pe.wait_ge(act_done, NACT * TILES * TILE_CHUNKS + CREDIT_ACT)
                b, o = slice(*PIECES[-1]), slice(k * 128, (k + 1) * 128)
                ps = dense_bank(n)[:, 0:b.stop - b.start]
                pe.matmul(ps, w1[:, 0, o], z1[:, b], start=True, stop=False)
                pe.matmul(ps, w1d[:, o], dense[:, b], start=False, stop=False)

            def dense_output(n):
                piece, k = divmod(n, OUTPUTS)
                lo, hi = PIECES[piece]
                b, w = slice(lo, hi), hi - lo
                ps = dense_bank(n)[:, 0:w]
                if n == 0:
                    pe.wait_ge(tail_in, 128)
                    pe.wait_ge(eT_ready, 2 * TILES)
                if n == DENSE_FIRST:
                    pe.wait_ge(z3_ready, TILES - 1)
                if 0 < n < BESIDE:
                    pe.wait_ge(mlp_act, n)
                if n >= BESIDE + RING:
                    pe.wait_ge(mlp_act, n - RING + 1)
                if k == 0:
                    tiles = -(-hi // TILE_B)
                    pe.wait_ge(z2_ready, tiles)
                    pe.wait_ge(z3_ready, tiles)
                if k < 4:
                    o = slice(k * 128, (k + 1) * 128)
                    if n < BESIDE:
                        pe.matmul(ps, w1[:, 0, o], z1[:, b], start=True, stop=False)
                        pe.matmul(ps, w1d[:, o], dense[:, b], start=False, stop=False)
                    pe.matmul(ps, w1[:, 1, o], z2[:, b], start=False, stop=False)
                    a = pe.matmul(ps, w1[:, 2, o], z3[:, b], start=False, stop=True)
                elif k < 6:
                    pe.wait_ge(mlp_act, OUTPUTS * piece + 4)
                    for i in range(4):
                        a = pe.matmul(ps, w2[:, i, (k - 4) * 128:(k - 3) * 128], h1[:, i, 0:w],
                                      start=i == 0, stop=i == 3)
                else:
                    pe.wait_ge(mlp_act, OUTPUTS * piece + 6)
                    for i in range(2):
                        a = pe.matmul(ps[0:1, :], w3[:, i:i + 1], h2[:, i, 0:w],
                                      start=i == 0, stop=i == 1)
                a.then_inc(mlp_ps, 1)

            def group(T, g, nxt, prep_next, first, zero, last):
                S = T * GROUPS + g

                def bank_work(s):
                    c, i = divmod(s, STEPS)
                    if s == 0:
                        pe.wait_ge(xL_ready, 2 * S + 1)
                    if s == 3 * STEPS:
                        pe.wait_ge(xL_ready, 2 * S + 2)
                    if not (first and s < RING):
                        wait_bank_free(pe, S, s)
                    x, w = slice(c * NC, (c + 1) * NC), slice(i * 512, (i + 1) * 512)
                    pe.matmul(Y[s % RING][:, :], xH[:, x], k1H[:, w], start=True, stop=False)
                    pe.matmul(Y[s % RING][:, :], xH[:, x], k1L[:, w], start=False, stop=False)
                    pe.matmul(Y[s % RING][:, :], xL[:, x], k1H[:, w], start=False,
                              stop=True).then_inc(y_dve if i in DVE_STEPS else y_act, 1)

                others = []
                for c in range(CHUNKS):
                    ch = g * CHUNKS + c - 2
                    if not (first and c < 2):
                        others.append((c * STEPS + MAKE_G, lambda c=c, ch=ch: make_G(
                            S * CHUNKS + c - 2, T if ch >= 0 else T - 1, ch % TILE_CHUNKS)))
                if not zero:
                    ms = np.linspace(0, M, Z3_TO - Z3_FROM + 1).astype(int).tolist()
                    for at, m0, m1 in zip(range(Z3_FROM, Z3_TO), ms, ms[1:]):
                        if at // GSTEPS == g:
                            others.append((at % GSTEPS, lambda m0=m0, m1=m1: z3_part(
                                T - 1, m0, m1, pP)))
                if prep_next:
                    for r, at in enumerate(PREP_AT):
                        others.append((at, lambda r=r: prep(T + 1, r)))
                if last:
                    for n, at in enumerate(DENSE_AT):
                        if min(at // GSTEPS, GROUPS - 1) == g:
                            others.append((at - g * GSTEPS, lambda n=n: dense_output(n)))
                if nxt:
                    for j, at in enumerate(PRODUCT_AT):
                        others.append((at + ADD, lambda j=j: add_block(S + 1, j)))
                in_steps(bank_work, others)

            def tile(T, first, last):
                for g in range(GROUPS):
                    end = g == GROUPS - 1
                    group(T, g, not (last and end), g == 2 and not last, first and g == 0, first,
                          last)

            pe.wait_ge(consts_in, 48)
            pe.wait_ge(gathered_most, 16 * MOST)
            for i in range(16):
                pe.matmul(pG[:, 0:128], ident[:, :], ident[:, :], start=True, stop=True)
            for r in range(4):
                prep(0, r, FIRST_PREP[r])
            pe.wait_ge(e_copied, 4)
            for i in range(1 + CHOSEN):
                choose(i)
            prep(0, 4, FIRST_PREP[4])
            prep(0, 5, FIRST_PREP[5])
            pe.wait_ge(k_ready, 1)
            for j in range(BLOCKS):
                add_block(0, j)
            pe.wait_ge(k_ready, 2)
            all_tiles(pe, tile)
            for ch in range(TILE_CHUNKS - 2, TILE_CHUNKS):
                make_G((TILES - 1) * TILE_CHUNKS + ch, TILES - 1, ch)
                for n in range(2):
                    dense_begin(BESIDE + 2 * (ch - TILE_CHUNKS + 2) + n)
            z3_part(TILES - 1, 0, M, pG)
            for n in range(BESIDE, OUTPUTS * len(PIECES)):
                dense_output(n)


def _constants():
    mask = (np.arange(128)[:, None] // D == np.arange(CHUNK_B)[None, :]).astype(np.float32)
    a, rep, j = np.arange(M), np.arange(REP), np.arange(CHOSEN)
    row = (a + rep[:, None] + REP * j[:, None, None]) % M
    row = np.concatenate([np.tile(a, REP), row.reshape(-1)])
    select = (np.arange(M)[:, None] == row).astype(np.float32)
    return np.eye(128, dtype=np.float32), mask, select


def kernel(**inputs):
    import concourse.bacc as bacc
    from concourse.bass_utils import run_bass_kernel_spmd

    x = {k: np.asarray(v) for k, v in inputs.items()}
    ident, mask, select = _constants()
    k0 = x["L0_rec_k0"]
    a = np.arange(M)
    k0a = np.zeros((BLOCKS, REP, M, H), np.float32)
    k0b = np.zeros((BLOCKS, REP, M, H), np.float32)
    for s in range(BLOCKS * REP):
        k0a[s // REP, s % REP] = k0[:, a, (a + s) % M].T
        if 0 < s < M // 2:
            k0b[s // REP, s % REP] = k0[:, (a + s) % M, a].T

    def by_row(k):
        return np.ascontiguousarray(k.transpose(1, 2, 0, 3).reshape(PR, BLOCKS * H))

    arrays = {
        "ids": x["ids"],
        **{f"tbl_{f}": x[f"tbl_{f}"] for f in range(TABLES)},
        "ident": ident, "mask": mask, "select": select,
        "k0a": by_row(k0a), "k0b": by_row(k0b),
        "k1": x["L0_rec_k1"].transpose(1, 2, 0).reshape(H, M * H),
        "k2": x["L0_rec_k2"].transpose(1, 2, 0),
        "w1": x["W_top1"][0:3 * H].reshape(3, H, 512).transpose(1, 0, 2),
        "w1d": x["W_top1"][3 * H:],
        "b1": x["b_top1"].reshape(4, 128).T,
        "w2": x["W_top2"].reshape(4, 128, 256).transpose(1, 0, 2),
        "b2": x["b_top2"].reshape(2, 128).T,
        "w3": x["W_top3"].reshape(2, 128).T,
        "dense": x["dense_ctx"].T,
    }
    arrays = {f"in_{k}": np.ascontiguousarray(v) for k, v in arrays.items()}
    nc = bacc.Bacc("TRN2", target_bir_lowering=False, num_devices=1)
    aps = {k: nc.dram_tensor(k, v.shape, mybir.dt.from_np(v.dtype), kind="ExternalInput").ap()
           for k, v in arrays.items()}
    out = nc.dram_tensor("out", (B, 1), mybir.dt.float32, kind="ExternalOutput").ap()
    names = ("ident", "mask", "select", "k0a", "k0b", "k1", "k2", "w1", "w1d", "b1", "w2", "b2",
             "w3", "dense")
    build(nc, aps["in_ids"], [aps[f"in_tbl_{f}"] for f in range(TABLES)],
          *[aps[f"in_{k}"] for k in names], out)
    r = run_bass_kernel_spmd(nc, [arrays], core_ids=[0])
    return r.results[0]["out"]
```
